# Optimizing a Trainium2 kernel written in Bass

```python
import numpy as np
import jax
import jax.numpy as jnp

def _softmax(x, axis=-1):
    return jax.nn.softmax(x, axis=axis)

def _gelu(x):
    return jax.nn.gelu(x, approximate=True)

def _silu(x):
    return jax.nn.silu(x)

def _sigmoid(x):
    return jax.nn.sigmoid(x)

def _layernorm(x, axis=-1, eps=1e-05):
    m = jnp.mean(x, axis=axis, keepdims=True)
    v = jnp.var(x, axis=axis, keepdims=True)
    return (x - m) / jnp.sqrt(v + eps)

def _scatter_add(tgt, idx, src, axis=0):
    return tgt.at[idx].add(src)

def _segment_sum(src, seg, n):
    return jax.ops.segment_sum(src, seg, n)
kernel_name = 'mk_decoder_postln_d1_seqx_r4_b4a2d5'

def setup_inputs(seed: int=0):
    np.random.seed(seed)
    _w = jnp.asarray

    def _rec_inputs():
        import jax
        import jax.numpy as jnp
        _rk = jax.random.key(seed)
        x = 7.22e-05 + 1 * jax.random.normal(jax.random.fold_in(_rk, 1), (32, 112, 256), jnp.float32)
        _lenS = 112 - jax.random.randint(jax.random.fold_in(_rk, 7), (32,), 0, max(1, 112 // 4) + 1, jnp.int32)
        _lenS2 = 375 - jax.random.randint(jax.random.fold_in(_rk, 8), (32,), 0, max(1, 375 // 4) + 1, jnp.int32)
        _ctx_1024P = jax.random.normal(jax.random.fold_in(_rk, 11), (32, 16, 256), jnp.float32)
        _ctx_1024c = jax.random.dirichlet(jax.random.fold_in(_rk, 511), 0.3 * jnp.ones((16,), jnp.float32), (32, 375))
        _ctx_1024t = jnp.einsum('bsk,bkd->bsd', _ctx_1024c, _ctx_1024P)
        _ctx_1024t = _ctx_1024t * jax.lax.rsqrt(jnp.mean(jnp.square(_ctx_1024t)) + 1e-12) * 0.953939
        ctx_1024 = 4.13588e-05 + 0.999923 * (_ctx_1024t + 0.3 * jax.random.normal(jax.random.fold_in(_rk, 611), (32, 375, 256), jnp.float32))
        _validS = jnp.arange(112)[None, :] < _lenS[:, None]
        _validS2 = jnp.arange(375)[None, :] < _lenS2[:, None]
        _causal = jnp.tril(jnp.ones((112, 112), dtype=bool))
        mask_Bx1xSxS2_bk1 = jnp.broadcast_to(_validS2[:, None, None, :], (32, 1, 112, 375))
        return (x, ctx_1024, mask_Bx1xSxS2_bk1)
    x, ctx_1024, mask_Bx1xSxS2_bk1 = _rec_inputs()

    def _L0_attn_setup():
        import jax, jax.numpy as jnp
        import numpy as np
        D_MODEL = 256
        THRESH = 0.01
        key = jax.random.key(seed)
        kx, kw = jax.random.split(key)
        x = jax.random.normal(kx, (4, 512, D_MODEL), dtype=jnp.float32)
        W = jax.random.normal(kw, (D_MODEL, D_MODEL), dtype=jnp.float32) / np.sqrt(D_MODEL)
        return {'x': x, 'W': W}
    _L0_attn_all = _L0_attn_setup()
    _L0_attn_in = {k: v for k, v in _L0_attn_all.items() if k in ('W',)}
    del _L0_attn_all

    def _L0_xattn_setup():
        import jax, jax.numpy as jnp
        import numpy as np
        B, S, D, H = (4, 512, 256, 16)
        HD = D // H
        key = jax.random.key(seed)
        ks = jax.random.split(key, 12)
        scale = 1.0 / np.sqrt(D)
        inp = {'queries': jax.random.normal(ks[0], (B, S, D), jnp.float32), 'keys': jax.random.normal(ks[1], (B, S, D), jnp.float32), 'values': jax.random.normal(ks[2], (B, S, D), jnp.float32), 'mask': jax.random.randint(ks[3], (B, 1, S, S), 0, 2).astype(bool), 'Wq': jax.random.normal(ks[4], (D, D), jnp.float32) * scale, 'bq': jnp.zeros((D,), jnp.float32), 'Wk': jax.random.normal(ks[5], (D, D), jnp.float32) * scale, 'bk': jnp.zeros((D,), jnp.float32), 'Wv': jax.random.normal(ks[6], (D, D), jnp.float32) * scale, 'bv': jnp.zeros((D,), jnp.float32), 'Wo': jax.random.normal(ks[7], (D, D), jnp.float32) * scale, 'bo': jnp.zeros((D,), jnp.float32)}
        return inp
    _L0_xattn_all = _L0_xattn_setup()
    _L0_xattn_in = {k: v for k, v in _L0_xattn_all.items() if k in ('Wq', 'bq', 'Wk', 'bk', 'Wv', 'bv', 'Wo', 'bo')}
    del _L0_xattn_all

    def _L0_ffn_setup():
        import jax, jax.numpy as jnp
        import numpy as np
        B, S, D, H, DOUT, E, K = (4, 512, 256, 256, 256, 8, 2)
        key = jax.random.key(seed)
        k1, k2, k3, k4 = jax.random.split(key, 4)
        x = jax.random.normal(k1, (B, S, D), dtype=jnp.float32)
        Wr = jax.random.normal(k2, (D, E), dtype=jnp.float32) * 0.02
        Wi = jax.random.normal(k3, (E, D, H), dtype=jnp.float32) * 0.02
        Wo = jax.random.normal(k4, (E, H, DOUT), dtype=jnp.float32) * 0.02
        return {'x': x, 'Wr': Wr, 'Wi': Wi, 'Wo': Wo}
    _L0_ffn_all = _L0_ffn_setup()
    _L0_ffn_in = {k: v for k, v in _L0_ffn_all.items() if k in ('Wr', 'Wi', 'Wo')}
    del _L0_ffn_all
    return {'x': x, 'ctx_1024': ctx_1024, 'mask_Bx1xSxS2_bk1': mask_Bx1xSxS2_bk1, 'L0_attn_W': _L0_attn_in['W'], 'L0_xattn_Wq': _L0_xattn_in['Wq'], 'L0_xattn_bq': _L0_xattn_in['bq'], 'L0_xattn_Wk': _L0_xattn_in['Wk'], 'L0_xattn_bk': _L0_xattn_in['bk'], 'L0_xattn_Wv': _L0_xattn_in['Wv'], 'L0_xattn_bv': _L0_xattn_in['bv'], 'L0_xattn_Wo': _L0_xattn_in['Wo'], 'L0_xattn_bo': _L0_xattn_in['bo'], 'L0_ffn_Wr': _L0_ffn_in['Wr'], 'L0_ffn_Wi': _L0_ffn_in['Wi'], 'L0_ffn_Wo': _L0_ffn_in['Wo']}

def reference(x, ctx_1024, mask_Bx1xSxS2_bk1, L0_attn_W, L0_xattn_Wq, L0_xattn_bq, L0_xattn_Wk, L0_xattn_bk, L0_xattn_Wv, L0_xattn_bv, L0_xattn_Wo, L0_xattn_bo, L0_ffn_Wr, L0_ffn_Wi, L0_ffn_Wo):
    import jax
    import jax.numpy as jnp

    def _L0_attn_ref(x, W):
        import jax, jax.numpy as jnp
        import numpy as np
        D_MODEL = 256
        THRESH = 0.01
        B, T, D = x.shape
        scale = 1.0 / jnp.sqrt(jnp.asarray(D, x.dtype))
        scores = jnp.einsum('btd,bsd->bts', x, x) * scale
        probs = jax.nn.softmax(scores, axis=-1)
        vacuum_mask = probs < THRESH
        vacuum_energy = jnp.where(vacuum_mask, probs, 0.0)
        vac_sum = vacuum_energy.sum(axis=-1, keepdims=True)
        vac_in = jnp.broadcast_to(vac_sum, (B, T, D))
        casimir = jnp.einsum('btd,od->bto', vac_in, W)
        sparse_probs = jnp.where(vacuum_mask, 0.0, probs)
        sparse_probs = sparse_probs / (sparse_probs.sum(axis=-1, keepdims=True) + 1e-09)
        attended = jnp.einsum('bts,bsd->btd', sparse_probs, x)
        return attended + casimir * 0.01

    def _L0_xattn_ref(queries, keys, values, mask, Wq, bq, Wk, bk, Wv, bv, Wo, bo):
        import jax, jax.numpy as jnp
        import numpy as np
        B, S, D, H = (4, 512, 256, 16)
        HD = D // H
        b, sq, d = queries.shape

        def split_heads(x):
            return x.reshape(b, x.shape[1], H, HD).transpose(0, 2, 1, 3)
        q = split_heads(queries @ Wq + bq)
        k = split_heads(keys @ Wk + bk)
        v = split_heads(values @ Wv + bv)
        scores = jnp.einsum('bhqd,bhkd->bhqk', q, k) / jnp.sqrt(jnp.float32(HD))
        scores = jnp.where(mask, jnp.float32(-1000000000000000.0), scores)
        attn = jax.nn.softmax(scores, axis=-1)
        ctx = jnp.einsum('bhqk,bhkd->bhqd', attn, v)
        ctx = ctx.transpose(0, 2, 1, 3).reshape(b, sq, d)
        return ctx @ Wo + bo

    def _L0_ffn_ref(x, Wr, Wi, Wo):
        import jax, jax.numpy as jnp
        import numpy as np
        B, S, D, H, DOUT, E, K = (4, 512, 256, 256, 256, 8, 2)
        b, s, d = x.shape
        e_cnt, _, h = Wi.shape
        dout = Wo.shape[2]
        xf = x.reshape(-1, d)
        T = xf.shape[0]
        probs = jax.nn.softmax(xf @ Wr, axis=-1)
        topk_p, topk_i = jax.lax.top_k(probs, K)
        mask = topk_i[:, :, None] == jnp.arange(e_cnt)[None, None, :]
        hmix = jnp.zeros((T, K, h), dtype=xf.dtype)
        for e in range(e_cnt):
            he = xf @ Wi[e]
            hmix = hmix + jnp.where(mask[:, :, e][:, :, None], he[:, None, :], 0.0)
        o = jnp.zeros((T, K, dout), dtype=xf.dtype)
        for e in range(e_cnt):
            oe = jnp.einsum('tkh,hd->tkd', hmix, Wo[e])
            o = o + jnp.where(mask[:, :, e][:, :, None], oe, 0.0)
        out = jnp.sum(o * topk_p[:, :, None], axis=1)
        return out.reshape(b, s, dout)
    x = _layernorm(x + _L0_attn_ref(x, L0_attn_W), axis=-1)
    x = _layernorm(x + _L0_xattn_ref(x, ctx_1024, ctx_1024, mask_Bx1xSxS2_bk1, L0_xattn_Wq, L0_xattn_bq, L0_xattn_Wk, L0_xattn_bk, L0_xattn_Wv, L0_xattn_bv, L0_xattn_Wo, L0_xattn_bo), axis=-1)
    x = _layernorm(x + _L0_ffn_ref(x, L0_ffn_Wr, L0_ffn_Wi, L0_ffn_Wo), axis=-1)
    return x

_drawn_inputs = setup_inputs


def setup_inputs(seed=0):
    import zlib

    import numpy as np

    out = dict(_drawn_inputs(seed))
    spreads = {'L0_xattn_bq': (0.0, 0.341),
     'L0_xattn_bk': (0.0, 0.8),
     'L0_xattn_bv': (0.0, 0.1),
     'L0_xattn_bo': (0.0, 0.1)}
    factors = {'L0_attn_W': 8.0}
    for name, (base, spread) in spreads.items():
        noise = np.random.default_rng([zlib.crc32(name.encode()), seed]).standard_normal(out[name].shape)
        drawn = base * np.exp(spread * noise) if base else spread * noise
        out[name] = jnp.asarray(drawn.astype(out[name].dtype))
    for name, factor in factors.items():
        out[name] = (out[name] * factor).astype(out[name].dtype)
    return out
```

```python
from contextlib import ExitStack

import concourse.bass as bass
from concourse import mybir

fp32, f32r, u8, u32 = mybir.dt.float32, mybir.dt.float32r, mybir.dt.uint8, mybir.dt.uint32
ALU = mybir.AluOpType
ACT = mybir.ActivationFunctionType
AX = mybir.AxisListType

BATCH, TOK, DIM, KEYS = 32, 112, 256, 375
HEADS, HEAD_DIM, EXPERTS = 16, 16, 8
KT = 3
KP = KEYS // KT
KEYS_EVEN = KEYS + KEYS % 2
DC = DIM // 128
PAIRS = 4
QUADS = HEADS // 4
SLOTS = HEADS + 3
BIG = 1e15
THRESH = 0.01
NEPS = 1e-5
SELF_SCALE = DIM ** -0.25
Q_SCALE = HEAD_DIM ** -0.5
RING = 4
TRING = 8
S_BANKS, T_BANK, O_BANK, G_BANK = (0, 1, 2), (3, 4), 5, (6, 7)

USES = [("xT", 0), ("rb", 1), ("Sc", 1), ("c0", 2), ("Wo", 3), ("c1", 4), ("PT", 5), ("x2T", 6),
        ("K0", 7), ("att", 8), ("K1", 9), ("lg", 10), ("x1T", 11), ("m0", 12), ("qT", 13),
        ("V0", 14), ("m1", 14), ("V1", 15), ("m2", 16), ("m3", 17)]
POST_USES = ("rb", "Wo", "x2T", "lg", "m0", "m1", "m2", "m3")


class Chain:

    def __init__(self, sem, names):
        self.sem, self.names, self.at = sem, list(names), 0

    def did(self, name, instruction):
        assert self.names[self.at] == name, (self.names[self.at], name)
        self.at = (self.at + 1) % len(self.names)
        instruction.then_inc(self.sem, 1)


def count(at, per, k):
    t, c = at
    return per * c + k if isinstance(t, int) else 2 * per * t + (per * c + k)


def wait(eng, sem, at, per, k):
    v = count(at, per, k)
    if not isinstance(v, int) or v > 0:
        eng.wait_ge(sem, v)


def wait_step(eng, chain, name, at):
    wait(eng, chain.sem, at, len(chain.names), chain.names.index(name) + 1)


def wait_turn(eng, sem, at, per):
    t, c = at
    turns = c // 2 + 1
    if isinstance(t, int):
        if turns > 0:
            eng.wait_ge(sem, 16 * per * turns)
    else:
        eng.wait_ge(sem, 16 * per * t + 16 * per * turns)


def shift(at, by):
    return at[0], at[1] + by


def row(at):
    t, c = at
    return c if isinstance(t, int) else 2 * t + c


def active(name, it):
    return 1 <= it <= BATCH if name in POST_USES else -1 <= it <= BATCH - 2


def previous_use(n, it):
    back, m = 0, n - 2
    while it + back >= -1:
        while m >= 0:
            name = USES[m][0]
            if active(name, it + back):
                return name, back + (-1 if name in POST_USES else 1)
            m -= 2
        back -= 1
        m = len(USES) - 2 + n % 2
    return None


def decoder_layer(nc, x, context, mask, attn_w, wq, bq, wk, bk, wv, bv, wo, bo, wr, wi, wout,
                  consts, out):
    ctx = ExitStack()
    with ctx:
        def sb(name, shape, dt=fp32):
            return ctx.enter_context(nc.sbuf_tensor(name, shape, dt))

        def sem(name):
            return ctx.enter_context(nc.semaphore(name))

        const_sb = sb("const_sb", [128, 128 + 2 + EXPERTS])
        ident = const_sb[:, 0:128]
        head_masks = const_sb[:, 128:130]
        expert_ids = const_sb[0:TOK, 130:130 + EXPERTS]
        ones = sb("ones", [128, TOK])
        wq_sb = sb("wq_sb", [128, DC, DIM])
        wk_sb = sb("wk_sb", [128, DC, DIM])
        wv_sb = sb("wv_sb", [128, DC, DIM])
        wo_sb = sb("wo_sb", [128, QUADS, DIM])
        attn_w_sb = sb("attn_w_sb", [128, DC, DIM])
        attn_wT = sb("attn_wT", [128, DC, DIM])
        w_sum = sb("w_sum", [TOK, DIM])
        bq_col = sb("bq_col", [128, DC])
        bk_col = sb("bk_col", [128, DC])
        bv_row = sb("bv_row", [128, DIM])
        bo_row = sb("bo_row", [TOK, DIM])
        wr_sb = sb("wr_sb", [128, DC, EXPERTS])
        wr_hi = sb("wr_hi", [128, DC, EXPERTS], f32r)
        wr_lo = sb("wr_lo", [128, DC, EXPERTS], f32r)
        wi_sb = sb("wi_sb", [128, 2, DC, DIM])
        wout_sb = sb("wout_sb", [128, 2, DC, DIM])
        wiT = sb("wiT", [128, 2, DC, DIM])
        we_hi = sb("we_hi", [128, DC, EXPERTS * DIM], f32r)
        we_lo = sb("we_lo", [128, DC, EXPERTS * DIM], f32r)

        x_sb = [sb(f"x_sb{k}", [TOK, DIM]) for k in range(2)]
        ctx_sb = [sb(f"ctx_sb{k}", [KP, KT, DIM]) for k in range(2)]
        mask_u8 = [sb(f"mask_u8{k}", [TOK, KEYS], u8) for k in range(2)]
        mask_add = [sb(f"mask_add{k}", [TOK, KT, KP]) for k in range(2)]
        xT = sb("xT", [128, DC, TOK])
        self_nmax = sb("self_nmax", [TOK, 1])
        self_sum = sb("self_sum", [TOK, 1])
        self_rsum = sb("self_rsum", [TOK, 1])
        self_exp = sb("self_exp", [TOK, TOK])
        self_p = sb("self_p", [TOK, TOK])
        sparse = sb("sparse", [TOK, TOK])
        vacuum = sb("vacuum", [TOK, TOK])
        sparse_sum = sb("sparse_sum", [TOK, 1])
        sparse_den = sb("sparse_den", [TOK, 1])
        sparse_r = sb("sparse_r", [TOK, 1])
        vac_sum = sb("vac_sum", [TOK, 1])
        vac_scaled = sb("vac_scaled", [TOK, 1])
        x_cas = sb("x_cas", [TOK, DIM])
        sparseT = sb("sparseT", [TOK, TOK])
        y1 = sb("y1", [TOK, DIM])
        x1 = sb("x1", [TOK, DIM])
        x1_bo = [sb(f"x1_bo{k}", [TOK, DIM]) for k in range(2)]
        x1T = sb("x1T", [128, DC, TOK])
        ctxT = sb("ctxT", [128, DC, KEYS])
        k_hi = sb("k_hi", [128, DC, KEYS], f32r)
        k_lo = sb("k_lo", [128, DC, KEYS], f32r)
        q_sb = sb("q_sb", [128, DC, TOK])
        q_hi = sb("q_hi", [128, DC, 2, TOK], f32r)
        q_lo = sb("q_lo", [128, DC, 2, TOK], f32r)
        stats = [sb(f"stats{n}", [TOK, 6]) for n in range(3)]
        moments = [sb(f"moments{n}", [TOK, 2]) for n in range(3)]
        minus_half = sb("minus_half", [TOK, 1])
        var_eps = [sb(f"var_eps{n}", [TOK, 1]) for n in range(3)]
        rstd = [sb(f"rstd{n}", [TOK, 1]) for n in range(3)]

        k_stack = [sb(f"k_stack{k}", [96, DC, PAIRS, KEYS_EVEN], f32r) for k in range(2)]
        q_stack = [sb(f"q_stack{k}", [96, DC, PAIRS, 2, TOK], f32r) for k in range(2)]
        v_sb = [sb(f"v_sb{k}", [KP, KT, HEADS, 32]) for k in range(2)]
        masked = sb("masked", [TOK, RING, KEYS])
        nmax = sb("nmax", [TOK, HEADS])
        probs = sb("probs", [TOK, RING, KEYS])
        probs_sum = [sb(f"probs_sum{k}", [TOK, HEADS]) for k in range(2)]
        probsT = sb("probsT", [KP, TRING, KT * TOK])

        rden = sb("rden", [TOK, HEADS])
        rden_wide = sb("rden_wide", [TOK, HEADS, 32])
        o_sb = sb("o_sb", [128, QUADS * TOK])
        attnT = sb("attnT", [128, QUADS * TOK])
        y2 = sb("y2", [TOK, DIM])
        x2 = sb("x2", [TOK, DIM])
        x2_hi = sb("x2_hi", [128, DC, TOK], f32r)
        x2_lo = sb("x2_lo", [128, DC, TOK], f32r)
        gate_nmax = sb("gate_nmax", [TOK, 1])
        gate_sum = sb("gate_sum", [TOK, 1])
        gate_r = sb("gate_r", [TOK, 1])
        gate_exp = sb("gate_exp", [TOK, EXPERTS])
        gate_p = sb("gate_p", [TOK, EXPERTS])
        top_p = sb("top_p", [TOK, 8])
        top_i = sb("top_i", [TOK, 8], u32)
        top_f = sb("top_f", [TOK, 8])
        gate_a = sb("gate_a", [TOK, EXPERTS])
        gate_b = sb("gate_b", [TOK, EXPERTS])
        gate = sb("gate", [TOK, EXPERTS])
        mix = sb("mix", [TOK, DIM])
        out_sb = [sb(f"out_sb{k}", [TOK, DIM]) for k in range(2)]

        psum = ctx.enter_context(nc.psum_tensor("psum", [128, 8, 512], fp32))
        bank_of = {name: psum[:, G_BANK[n % 2], :] for n, (name, _) in enumerate(USES)}
        o_bank = psum[:, O_BANK, :]

        consts_in, weights_in, wi_in = sem("consts_in"), sem("weights_in"), [sem("wi_in0"), sem("wi_in1")]
        x_in = [sem(f"x_in{k}") for k in range(2)]
        ctx_in = [sem(f"ctx_in{k}") for k in range(2)]
        mask_in = [sem(f"mask_in{k}") for k in range(2)]
        k_stacked = [sem(f"k_stacked{k}") for k in range(2)]
        q_stacked = [sem(f"q_stacked{k}") for k in range(2)]
        out_written = [sem(f"out_written{k}") for k in range(2)]
        setup_dve, setup_pe = sem("setup_dve"), sem("setup_pe")
        setup_pool, waits_passed = sem("setup_pool"), sem("waits_passed")
        wiT_ready, wiT_copied = sem("wiT_ready"), sem("wiT_copied")
        we_ready, we_split = sem("we_ready"), sem("we_split")
        scores_ready, masked_ready = sem("scores_ready"), sem("masked_ready")
        probs_ready, probsT_ready = sem("probs_ready"), sem("probsT_ready")
        probsT_copied, pv_done = sem("probsT_copied"), sem("pv_done")
        pe_pre = Chain(sem("pe_pre"), [u for u, _ in USES if u not in POST_USES])
        pe_post = Chain(sem("pe_post"), POST_USES)
        act_pre = Chain(sem("act_pre"), ["self_exp", "c0", "sparseT", "k_hi0", "k_hi1", "x1T", "q0", "q1"])
        act_post = Chain(sem("act_post"), ["o_sb", "x2_hi", "gate_exp"])
        dve_pre = Chain(sem("dve_pre"), [
            "xT", "self_max", "self_rsum", "self_p", "sparse", "vacuum", "sparse_den", "c1",
            "sparse_r", "vac_scaled", "x_cas", "k_lo0", "y1", "stats", "moments", "k_lo1", "x1",
            "q_hi0", "q_hi1", "q_lo0", "q_lo1", "v0", "v1", "v2"])
        dve_post = Chain(sem("dve_post"), [
            "rden", "rden_wide", "attnT", "y2", "stats2", "moments2", "x2", "x2_lo", "gate_max", "gate_r",
            "gate_p", "top_p", "top_i", "top_f", "gate_a", "gate_b", "gate"]
            + [f"e{e}" for e in range(EXPERTS)] + ["stats3", "moments3", "out"])
        pool_pre = Chain(sem("pool_pre"), ["mask", "var1", "rstd1", "x1_bo"])
        pool_post = Chain(sem("pool_post"), ["var2", "rstd2", "var3", "rstd3"])
        taken = {"xT": (dve_pre, "xT"), "Sc": (act_pre, "self_exp"), "c0": (act_pre, "c0"),
                 "c1": (dve_pre, "c1"), "PT": (act_pre, "sparseT"), "K0": (dve_pre, "k_lo0"),
                 "att": (dve_pre, "y1"), "K1": (dve_pre, "k_lo1"), "x1T": (act_pre, "x1T"),
                 "qT": (act_pre, "q1"), "V0": (dve_pre, "v1"), "V1": (dve_pre, "v2"),
                 "rb": (dve_post, "attnT"), "Wo": (dve_post, "y2"), "x2T": (dve_post, "x2_lo"),
                 "lg": (act_post, "gate_exp"), "m0": (dve_post, "e1"), "m1": (dve_post, "e3"),
                 "m2": (dve_post, "e5"), "m3": (dve_post, "e7")}

        def settle(eng):
            eng.sem_inc(waits_passed, 1)

        def run(eng, iteration):
            for c in (-1, 0, 1):
                iteration((0, c), c)
            with eng.Fori(1, BATCH // 2 - 1) as t:
                iteration((t, 0), 2)
                iteration((t, 1), 3)
            for c in (BATCH - 2, BATCH - 1, BATCH):
                iteration((0, c), c)

        def stages(it):
            return -1 <= it <= BATCH - 2, 0 <= it <= BATCH - 1, 1 <= it <= BATCH

        block = ctx.enter_context(nc.Block())

        @block.sync
        def _(sp):
            def load(at):
                k = at[1] % 2
                sp.dma_start(x_sb[k][:, :], x[row(at)]).then_inc(x_in[k], 16)
                sp.dma_start(ctx_sb[k][:, :, :], context[row(at)].rearrange("(p j) d -> p j d", j=KT))\
                  .then_inc(ctx_in[k], 16)
                sp.dma_start(mask_u8[k][:, :], mask[row(at)]).then_inc(mask_in[k], 16)

            sp.dma_start(const_sb[:, :], consts).then_inc(consts_in, 16)
            load((0, 0))
            sp.dma_start(attn_w_sb[:, :, :], attn_w.rearrange("(c p) n -> p c n", p=128)).then_inc(weights_in, 16)
            for dst, src in ((wk_sb, wk), (wv_sb, wv), (wq_sb, wq), (wr_sb, wr)):
                sp.dma_start(dst[:, :, :], src.rearrange("(c p) n -> p c n", p=128)).then_inc(weights_in, 16)
            sp.dma_start(bq_col[:, :], bq.rearrange("(c p) -> p c", p=128), allow_slow_non_contiguous=True).then_inc(weights_in, 16)
            sp.dma_start(bk_col[:, :], bk.rearrange("(c p) -> p c", p=128), allow_slow_non_contiguous=True).then_inc(weights_in, 16)
            sp.dma_start(bv_row[:, :], bv.rearrange("(a n) -> a n", a=1).broadcast_to([128, DIM])).then_inc(weights_in, 16)
            sp.dma_start(bo_row[:, :], bo.rearrange("(a n) -> a n", a=1).broadcast_to([TOK, DIM])).then_inc(weights_in, 16)
            sp.wait_ge(setup_dve, 3)
            for j in range(4):
                sp.dma_start(wo_sb[32 * j:32 * j + HEAD_DIM, :, :],
                             wo.rearrange("(r j d) n -> j d r n", j=4, d=HEAD_DIM)[j]).then_inc(weights_in, 16)
            load((0, 1))
            for e in range(EXPERTS):
                if e >= 2:
                    sp.wait_ge(we_ready, e - 1)
                sp.dma_start(wi_sb[:, e % 2, :, :], wi[e].rearrange("(c p) n -> p c n", p=128)).then_inc(wi_in[e % 2], 16)
                sp.dma_start(wout_sb[:, e % 2, :, :], wout[e].rearrange("(c p) n -> p c n", p=128)).then_inc(wi_in[e % 2], 16)

            def iteration(at, it):
                pre, attn, post = stages(it)
                p, o, k = shift(at, 1), shift(at, -1), at[1] % 2
                if 0 <= it <= BATCH - 3:
                    wait_step(sp, dve_pre, "x1", at)
                    settle(sp)
                    wait_step(sp, pe_pre, "V1", at)
                    settle(sp)
                    wait_step(sp, pool_pre, "mask", at)
                    settle(sp)
                    load(shift(at, 2))
                if pre:
                    wait_step(sp, act_pre, "k_hi1", p)
                    settle(sp)
                    wait_step(sp, dve_pre, "k_lo1", p)
                    settle(sp)
                    wait(sp, scores_ready, o, HEADS, HEADS)
                    settle(sp)
                    for g, part in enumerate((k_hi, k_lo, k_hi)):
                        for a in range(PAIRS):
                            sp.dma_start(k_stack[1 - k][32 * g:32 * g + 32, :, a, 0:KEYS].bitcast(fp32),
                                         part[32 * a:32 * a + 32, :, :].bitcast(fp32)).then_inc(k_stacked[1 - k], 16)
                    wait_step(sp, dve_pre, "q_lo1", p)
                    settle(sp)
                    for g, part in enumerate((q_hi, q_hi, q_lo)):
                        for a in range(PAIRS):
                            sp.dma_start(q_stack[1 - k][32 * g:32 * g + 32, :, a, :, :].bitcast(fp32),
                                         part[32 * a:32 * a + 32, :, :, :].bitcast(fp32)).then_inc(q_stacked[1 - k], 16)
                if post:
                    wait_step(sp, dve_post, "out", o)
                    settle(sp)
                    sp.dma_start(out[row(o)], out_sb[1 - k][:, :]).then_inc(out_written[1 - k], 16)

            run(sp, iteration)
            for k in range(2):
                sp.wait_ge(out_written[k], 16 * BATCH // 2)

        @block.gpsimd
        def _(pool):
            nc.gpsimd.memset(minus_half[:, :], -0.5).then_inc(setup_pool, 1)
            pool.wait_ge(setup_pool, 1)

            def inverse_deviation(n, chain, batch):
                settle(pool)
                chain.did(f"var{n}", nc.gpsimd.tensor_scalar(
                    var_eps[n - 1][:, :], moments[n - 1][:, 1:2], NEPS, None, ALU.add))
                wait_step(pool, chain, f"var{n}", batch)
                chain.did(f"rstd{n}", nc.gpsimd.tensor_tensor(
                    rstd[n - 1][:, :], var_eps[n - 1][:, :], minus_half[:, :], ALU.pow))

            def iteration(at, it):
                pre, attn, post = stages(it)
                p, o, k = shift(at, 1), shift(at, -1), at[1] % 2
                if pre:
                    wait_turn(pool, mask_in[1 - k], p, 1)
                    wait(pool, masked_ready, o, HEADS, HEADS)
                    settle(pool)
                    pool_pre.did("mask", nc.gpsimd.tensor_scalar(
                        mask_add[1 - k][:, :, :], mask_u8[1 - k][:, :].rearrange("t (p j) -> t j p", j=KT),
                        BIG, None, ALU.mult))
                if post:
                    wait_step(pool, dve_post, "moments2", o)
                    inverse_deviation(2, pool_post, o)
                if pre:
                    wait_step(pool, dve_pre, "moments", p)
                    inverse_deviation(1, pool_pre, p)
                    wait_step(pool, dve_pre, "x1", p)
                    wait_step(pool, dve_post, "y2", o)
                    if it == -1:
                        pool.wait_ge(weights_in, 16 * 13)
                    pool_pre.did("x1_bo", nc.gpsimd.tensor_tensor(
                        x1_bo[1 - k][:, :], x1[:, :], bo_row[:, :], ALU.add))
                if post:
                    wait_step(pool, dve_post, "moments3", o)
                    inverse_deviation(3, pool_post, o)

            run(pool, iteration)

        @block.scalar
        def _(act):
            def iteration(at, it):
                pre, attn, post = stages(it)
                p, o, k = shift(at, 1), shift(at, -1), at[1] % 2
                for n in range(SLOTS):
                    if post and n == 0:
                        wait(act, pv_done, o, QUADS, QUADS)
                        act_post.did("o_sb", nc.scalar.activation(o_sb[:, :], o_bank[:, 0:QUADS * TOK], ACT.Copy))
                    if attn and n < HEADS:
                        wait(act, masked_ready, at, HEADS, n + 1)
                        wait(act, probsT_ready, at, HEADS, n - RING + 1)
                        nc.scalar.activation(probs[:, n % RING, :], masked[:, n % RING, :], ACT.Exp,
                                             bias=nmax[:, n:n + 1], scale=-1.0,
                                             accum_out=probs_sum[k][:, n:n + 1]).then_inc(probs_ready, 1)
                    if attn and 2 <= n < HEADS + 2:
                        h = n - 2
                        wait(act, probsT_ready, at, HEADS, h + 1)
                        wait(act, pv_done, at, QUADS, h // 4 - 1)
                        nc.scalar.activation(probsT[:, h % TRING, :], psum[0:KP, T_BANK[h % 2], 0:KT * TOK],
                                             ACT.Copy).then_inc(probsT_copied, 1)
                    if pre and n == 2:
                        wait_step(act, dve_pre, "self_max", p)
                        act_pre.did("self_exp", nc.scalar.activation(
                            self_exp[:, :], bank_of["Sc"][0:TOK, 0:TOK], ACT.Exp, bias=self_nmax[:, :],
                            scale=1.0, accum_out=self_sum[:, :]))
                        wait_step(act, pe_pre, "c0", p)
                        act_pre.did("c0", nc.scalar.activation(ctxT[:, 0, :], bank_of["c0"][:, 0:KEYS], ACT.Copy))
                    if pre and n == 5:
                        wait_step(act, pe_pre, "PT", p)
                        act_pre.did("sparseT", nc.scalar.activation(
                            sparseT[:, :], bank_of["PT"][0:TOK, 0:TOK], ACT.Copy))
                    if post and n == 6:
                        wait_step(act, pe_post, "x2T", o)
                        act_post.did("x2_hi", nc.scalar.activation(
                            x2_hi[:, :, :].rearrange("p c t -> p (c t)"), bank_of["x2T"][:, 0:DC * TOK], ACT.Copy))
                    if pre and n in (7, 9):
                        c = (n - 7) // 2
                        wait_step(act, pe_pre, f"K{c}", p)
                        if c == 0:
                            wait_turn(act, k_stacked[k], at, 12)
                        act_pre.did(f"k_hi{c}", nc.scalar.activation(
                            k_hi[:, c, :], bank_of[f"K{c}"][:, 0:KEYS], ACT.Identity, bias=bk_col[:, c:c + 1]))
                    if post and n == 10:
                        wait_step(act, dve_post, "gate_max", o)
                        act_post.did("gate_exp", nc.scalar.activation(
                            gate_exp[:, :], bank_of["lg"][0:TOK, 0:EXPERTS], ACT.Exp, bias=gate_nmax[:, :],
                            scale=1.0, accum_out=gate_sum[:, :]))
                    if pre and n == 11:
                        wait_step(act, pe_pre, "x1T", p)
                        act_pre.did("x1T", nc.scalar.activation(
                            x1T[:, :, :].rearrange("p c t -> p (c t)"), bank_of["x1T"][:, 0:DC * TOK], ACT.Copy))
                    if pre and n == 13:
                        wait_step(act, pe_pre, "qT", p)
                        for c in range(DC):
                            act_pre.did(f"q{c}", nc.scalar.activation(
                                q_sb[:, c, :], bank_of["qT"][:, c * TOK:(c + 1) * TOK], ACT.Identity,
                                bias=bq_col[:, c:c + 1]))

            act.wait_ge(weights_in, 16 * 13)
            run(act, iteration)

        @block.vector
        def _(dve):
            nc.vector.memset(v_sb[0][:, :, :, :], 0.0).then_inc(setup_dve, 1)
            nc.vector.memset(ones[:, :], 1.0).then_inc(setup_dve, 1)
            nc.vector.memset(wo_sb[:, :, :], 0.0).then_inc(setup_dve, 1)
            nc.vector.memset(v_sb[1][:, :, :, :], 0.0)
            for k in range(2):
                nc.vector.memset(k_stack[k][:, :, :, KEYS:KEYS_EVEN].bitcast(fp32), 0.0)
            dve.wait_ge(weights_in, 16 * 13)
            for c in range(DC):
                dve.wait_ge(setup_pe, c + 1)
                nc.vector.tensor_copy(attn_wT[:, c, :], psum[:, c, 0:DIM]).then_inc(setup_dve, 1)
            dve.wait_ge(setup_pe, DC + 1)
            nc.vector.tensor_copy(w_sum[:, :], psum[0:TOK, 2, 0:DIM]).then_inc(setup_dve, 1)
            nc.vector.tensor_copy(wr_hi[:, :, :], wr_sb[:, :, :]).then_inc(setup_dve, 1)
            dve.wait_ge(setup_dve, 7)
            nc.vector.tensor_tensor(wr_lo[:, :, :], wr_sb[:, :, :], wr_hi[:, :, :].bitcast(fp32), ALU.subtract)\
              .then_inc(setup_dve, 1)

            def expert_weights():
                for e in range(EXPERTS):
                    dve.wait_ge(wiT_ready, e + 1)
                    nc.vector.tensor_copy(wiT[:, e % 2, :, :], psum[:, 0, :].rearrange("p (c n) -> p c n", c=DC))\
                      .then_inc(wiT_copied, 1)
                    dve.wait_ge(we_ready, e + 1)
                    prod = psum[:, 1 + e % 2, :].rearrange("p (c n) -> p c n", c=DC)
                    hi = we_hi[:, :, e * DIM:(e + 1) * DIM]
                    nc.vector.tensor_copy(hi, prod).then_inc(we_split, 1)
                    dve.wait_ge(we_split, 2 * e + 1)
                    nc.vector.tensor_tensor(we_lo[:, :, e * DIM:(e + 1) * DIM], prod, hi.bitcast(fp32), ALU.subtract)\
                      .then_inc(we_split, 1)

            def iteration(at, it):
                pre, attn, post = stages(it)
                p, o, k = shift(at, 1), shift(at, -1), at[1] % 2

                def after(chain, name, batch):
                    wait_step(dve, chain, name, batch)

                def head(n):
                    wait(dve, scores_ready, at, HEADS, n + 1)
                    wait(dve, probs_ready, at, HEADS, n - RING + 1)
                    if n == 0:
                        wait_step(dve, pool_pre, "mask", at)
                    settle(dve)
                    nc.vector.tensor_tensor_reduce(
                        masked[:, n % RING, :], psum[0:TOK, S_BANKS[n % 3], 0:KEYS],
                        mask_add[k][:, :, :].rearrange("t j p -> t (j p)"), 1.0, 3.0e38, ALU.add, ALU.min,
                        nmax[:, n:n + 1]).then_inc(masked_ready, 1)

                for n in range(SLOTS):
                    if post and n == 0:
                        wait(dve, probs_ready, o, HEADS, HEADS)
                        dve_post.did("rden", nc.vector.reciprocal(rden[:, :], probs_sum[1 - k][:, :]))
                        after(dve_post, "rden", o)
                        dve_post.did("rden_wide", nc.vector.tensor_copy(
                            rden_wide[:, :, :], rden[:, :].unsqueeze(2).broadcast_to([TOK, HEADS, 32])))
                    if attn and n < HEADS:
                        head(n)
                    if pre and n == 0:
                        after(pe_pre, "xT", p)
                        dve_pre.did("xT", nc.vector.tensor_scalar(
                            xT[:, :, :].rearrange("p c t -> p (c t)"), bank_of["xT"][:, 0:DC * TOK],
                            SELF_SCALE, None, ALU.mult))
                    if post and n == 1:
                        after(pe_post, "rb", o)
                        after(act_post, "o_sb", o)
                        dve_post.did("attnT", nc.vector.tensor_tensor(
                            attnT[:, :], o_sb[:, :], bank_of["rb"][:, 0:QUADS * TOK], ALU.mult))
                    if pre and n == 1:
                        after(pe_pre, "Sc", p)
                        dve_pre.did("self_max", nc.vector.tensor_reduce(
                            self_nmax[:, :], bank_of["Sc"][0:TOK, 0:TOK], AX.X, ALU.max, negate=True))
                    if pre and n == 2:
                        after(act_pre, "self_exp", p)
                        dve_pre.did("self_rsum", nc.vector.reciprocal(self_rsum[:, :], self_sum[:, :]))
                        after(dve_pre, "self_rsum", p)
                        dve_pre.did("self_p", nc.vector.tensor_scalar(
                            self_p[:, :], self_exp[:, :], self_rsum[:, :], None, ALU.mult))
                    if pre and n == 3:
                        after(dve_pre, "self_p", p)
                        dve_pre.did("sparse", nc.vector.scalar_tensor_tensor(
                            out=sparse[:, :], in0=self_p[:, :], scalar=THRESH, in1=self_p[:, :],
                            op0=ALU.is_ge, op1=ALU.mult, accum_out=sparse_sum[:, :]))
                        dve_pre.did("vacuum", nc.vector.scalar_tensor_tensor(
                            out=vacuum[:, :], in0=self_p[:, :], scalar=THRESH, in1=self_p[:, :],
                            op0=ALU.is_lt, op1=ALU.mult, accum_out=vac_sum[:, :]))
                    if post and n == 4:
                        after(pe_post, "Wo", o)
                        after(pool_pre, "x1_bo", o)
                        dve_post.did("y2", nc.vector.tensor_tensor(
                            y2[:, :], bank_of["Wo"][0:TOK, 0:DIM], x1_bo[1 - k][:, :], ALU.add))
                        after(dve_post, "y2", o)
                        dve_post.did("stats2", nc.vector.bn_stats(stats[1][:, :], y2[:, :]))
                    if pre and n == 4:
                        after(dve_pre, "vacuum", p)
                        dve_pre.did("sparse_den", nc.vector.tensor_scalar(
                            sparse_den[:, :], sparse_sum[:, :], 1e-9, None, ALU.add))
                    if post and n == 5:
                        after(dve_post, "stats2", o)
                        settle(dve)
                        dve_post.did("moments2", nc.vector.bn_aggr(moments[1][:, :], stats[1][:, :]))
                    if pre and n == 5:
                        after(pe_pre, "c1", p)
                        dve_pre.did("c1", nc.vector.tensor_copy(ctxT[:, 1, :], bank_of["c1"][:, 0:KEYS]))
                        after(dve_pre, "sparse_den", p)
                        dve_pre.did("sparse_r", nc.vector.reciprocal(sparse_r[:, :], sparse_den[:, :]))
                        dve_pre.did("vac_scaled", nc.vector.tensor_scalar(
                            vac_scaled[:, :], vac_sum[:, :], 0.01, None, ALU.mult))
                    if post and n == 5:
                        after(pool_post, "rstd2", o)
                        dve_post.did("x2", nc.vector.tensor_scalar(
                            x2[:, :], y2[:, :], moments[1][:, 0:1], rstd[1][:, :], ALU.subtract, ALU.mult))
                    if pre and n == 6:
                        after(dve_pre, "vac_scaled", p)
                        dve_pre.did("x_cas", nc.vector.scalar_tensor_tensor(
                            out=x_cas[:, :], in0=w_sum[:, :], scalar=vac_scaled[:, :], in1=x_sb[1 - k][:, :],
                            op0=ALU.mult, op1=ALU.add))
                    if post and n == 7:
                        after(act_post, "x2_hi", o)
                        dve_post.did("x2_lo", nc.vector.tensor_tensor(
                            x2_lo[:, :, :].rearrange("p c t -> p (c t)"), bank_of["x2T"][:, 0:DC * TOK],
                            x2_hi[:, :, :].rearrange("p c t -> p (c t)").bitcast(fp32), ALU.subtract))
                    if pre and n in (8, 10):
                        c = (n - 8) // 2
                        if c == 1:
                            after(dve_pre, "stats", p)
                            settle(dve)
                            dve_pre.did("moments", nc.vector.bn_aggr(moments[0][:, :], stats[0][:, :]))
                        after(act_pre, f"k_hi{c}", p)
                        dve_pre.did(f"k_lo{c}", nc.vector.scalar_tensor_tensor(
                            out=k_lo[:, c, :], in0=bank_of[f"K{c}"][:, 0:KEYS], scalar=bk_col[:, c:c + 1],
                            in1=k_hi[:, c, :].bitcast(fp32), op0=ALU.add, op1=ALU.subtract))
                    if pre and n == 9:
                        after(pe_pre, "att", p)
                        after(dve_pre, "x_cas", p)
                        dve_pre.did("y1", nc.vector.scalar_tensor_tensor(
                            out=y1[:, :], in0=bank_of["att"][0:TOK, 0:DIM], scalar=sparse_r[:, :],
                            in1=x_cas[:, :], op0=ALU.mult, op1=ALU.add))
                        after(dve_pre, "y1", p)
                        dve_pre.did("stats", nc.vector.bn_stats(stats[0][:, :], y1[:, :]))
                    if post and n == 10:
                        after(pe_post, "lg", o)
                        dve_post.did("gate_max", nc.vector.tensor_reduce(
                            gate_nmax[:, :], bank_of["lg"][0:TOK, 0:EXPERTS], AX.X, ALU.max, negate=True))
                    if pre and n == 10:
                        after(pool_pre, "rstd1", p)
                        after(pool_pre, "x1_bo", at)
                        dve_pre.did("x1", nc.vector.tensor_scalar(
                            x1[:, :], y1[:, :], moments[0][:, 0:1], rstd[0][:, :], ALU.subtract, ALU.mult))
                    if post and n == 11:
                        after(act_post, "gate_exp", o)
                        dve_post.did("gate_r", nc.vector.reciprocal(gate_r[:, :], gate_sum[:, :]))
                        after(dve_post, "gate_r", o)
                        dve_post.did("gate_p", nc.vector.tensor_scalar(
                            gate_p[:, :], gate_exp[:, :], gate_r[:, :], None, ALU.mult))
                    if post and n == 12:
                        after(dve_post, "gate_p", o)
                        settle(dve)
                        dve_post.did("top_p", nc.vector.max(top_p[:, :], gate_p[:, :]))
                        after(dve_post, "top_p", o)
                        settle(dve)
                        dve_post.did("top_i", nc.vector.max_index(top_i[:, :], top_p[:, :], gate_p[:, :]))
                        after(dve_post, "top_i", o)
                        dve_post.did("top_f", nc.vector.tensor_copy(top_f[:, :], top_i[:, :]))
                    if post and n == 13:
                        after(dve_post, "top_f", o)
                        dve_post.did("gate_a", nc.vector.tensor_scalar(
                            gate_a[:, :], expert_ids, top_f[:, 0:1], top_p[:, 0:1], ALU.is_equal, ALU.mult))
                        dve_post.did("gate_b", nc.vector.tensor_scalar(
                            gate_b[:, :], expert_ids, top_f[:, 1:2], top_p[:, 1:2], ALU.is_equal, ALU.mult))
                        after(dve_post, "gate_b", o)
                        dve_post.did("gate", nc.vector.tensor_tensor(
                            gate[:, :], gate_a[:, :], gate_b[:, :], ALU.add))
                    if pre and n == 14:
                        after(act_pre, "q1", p)
                        wait_turn(dve, q_stacked[k], at, 12)
                        for half in range(2):
                            dve_pre.did(f"q_hi{half}", nc.vector.tensor_scalar(
                                q_hi[:, :, half, :], q_sb[:, :, :], head_masks[:, half:half + 1], None, ALU.mult))
                        after(dve_pre, "q_hi1", p)
                        for half in range(2):
                            dve_pre.did(f"q_lo{half}", nc.vector.scalar_tensor_tensor(
                                out=q_lo[:, :, half, :], in0=q_sb[:, :, :], scalar=head_masks[:, half:half + 1],
                                in1=q_hi[:, :, half, :].bitcast(fp32), op0=ALU.mult, op1=ALU.subtract))
                    if pre and n in (15, 16):
                        after(pe_pre, f"V{n - 15}", p)
                        for j in ((0, 1), (2,))[n - 15]:
                            dve_pre.did(f"v{j}", nc.vector.tensor_tensor(
                                v_sb[1 - k][:, j, :, 0:HEAD_DIM],
                                bank_of[f"V{n - 15}"][0:KP, (j % 2) * DIM:(j % 2 + 1) * DIM].rearrange(
                                    "p (h d) -> p h d", d=HEAD_DIM),
                                bv_row[0:KP, :].rearrange("p (h d) -> p h d", d=HEAD_DIM), ALU.add))
                    if post and n in (13, 15, 16, 17):
                        m = (13, 15, 16, 17).index(n)
                        after(pe_post, f"m{m}", o)
                        for e in (2 * m, 2 * m + 1):
                            after(dve_post, f"e{e - 1}" if e else "gate", o)
                            dve_post.did(f"e{e}", nc.vector.scalar_tensor_tensor(
                                out=mix[:, :], in0=bank_of[f"m{m}"][0:TOK, (e % 2) * DIM:(e % 2 + 1) * DIM],
                                scalar=gate[:, e:e + 1], in1=(mix if e else x2)[:, :], op0=ALU.mult, op1=ALU.add))
                    if post and n == 18:
                        after(dve_post, f"e{EXPERTS - 1}", o)
                        dve_post.did("stats3", nc.vector.bn_stats(stats[2][:, :], mix[:, :]))
                        after(dve_post, "stats3", o)
                        settle(dve)
                        dve_post.did("moments3", nc.vector.bn_aggr(moments[2][:, :], stats[2][:, :]))
                        after(pool_post, "rstd3", o)
                        wait_turn(dve, out_written[k], shift(o, -1), 1)
                        dve_post.did("out", nc.vector.tensor_scalar(
                            out_sb[1 - k][:, :], mix[:, :], moments[2][:, 0:1], rstd[2][:, :],
                            ALU.subtract, ALU.mult))
                if it == -1:
                    expert_weights()

            run(dve, iteration)

        @block.tensor
        def _(pe):
            pe.wait_ge(consts_in, 16)
            pe.wait_ge(weights_in, 16 * 13)
            for c in range(DC):
                for r in range(DC):
                    mm = nc.tensor.transpose(psum[:, c, r * 128:(r + 1) * 128],
                                             attn_w_sb[:, r, c * 128:(c + 1) * 128], ident)
                mm.then_inc(setup_pe, 1)
            pe.wait_ge(setup_dve, 5)
            for c in range(DC):
                mm = nc.tensor.matmul(psum[0:TOK, 2, 0:DIM], ones[:, :], attn_wT[:, c, :],
                                      start=(c == 0), stop=(c == DC - 1))
            mm.then_inc(setup_pe, 1)

            def expert_weights():
                for e in range(EXPERTS):
                    pe.wait_ge(wi_in[e % 2], 32 * (e // 2 + 1))
                    if e:
                        pe.wait_ge(wiT_copied, e)
                    for c in range(DC):
                        for r in range(DC):
                            mm = nc.tensor.transpose(
                                psum[:, 0, c * DIM + r * 128:c * DIM + (r + 1) * 128],
                                wi_sb[:, e % 2, r, c * 128:(c + 1) * 128], ident)
                    mm.then_inc(wiT_ready, 1)
                    pe.wait_ge(wiT_copied, e + 1)
                    if e >= 2:
                        pe.wait_ge(we_split, 2 * (e - 1))
                    for r in range(DC):
                        for c in range(DC):
                            mm = nc.tensor.matmul(
                                psum[:, 1 + e % 2, r * DIM:(r + 1) * DIM],
                                wiT[:, e % 2, c, r * 128:(r + 1) * 128], wout_sb[:, e % 2, c, :],
                                start=(c == 0), stop=(c == DC - 1))
                    mm.then_inc(we_ready, 1)

            def iteration(at, it):
                pre, attn, post = stages(it)
                p, o, k = shift(at, 1), shift(at, -1), at[1] % 2

                def scores(n):
                    if n == 0:
                        wait_turn(pe, k_stacked[k], at, 12)
                        wait_turn(pe, q_stacked[k], at, 12)
                    if n >= 3:
                        wait(pe, masked_ready, at, HEADS, n - 2)
                    else:
                        wait(pe, masked_ready, shift(at, -1), HEADS, HEADS)
                    pair = n // 2
                    nc.tensor.matmul(psum[0:TOK, S_BANKS[n % 3], 0:KEYS_EVEN],
                                     q_stack[k][:, pair // PAIRS, pair % PAIRS, n % 2, :],
                                     k_stack[k][:, pair // PAIRS, pair % PAIRS, :],
                                     start=True, stop=True).then_inc(scores_ready, 1)

                def transpose_probs(n):
                    wait(pe, probs_ready, at, HEADS, n + 1)
                    wait(pe, probsT_copied, at, HEADS, n - 1)
                    for j in range(KT):
                        mm = nc.tensor.transpose(psum[0:KP, T_BANK[n % 2], j * TOK:(j + 1) * TOK],
                                                 probs[:, n % RING, j * KP:(j + 1) * KP], ident[0:TOK, 0:TOK])
                    mm.then_inc(probsT_ready, 1)

                def weigh_values(r):
                    wait(pe, probsT_copied, at, HEADS, 4 * r + 4)
                    if r == 0:
                        wait_step(pe, dve_pre, "v2", at)
                        wait_step(pe, act_post, "o_sb", shift(at, -1))
                    for t in range(KT):
                        for j in range(4):
                            h = 4 * r + j
                            mm = nc.tensor.matmul(
                                o_bank[32 * j:32 * j + 32, r * TOK:(r + 1) * TOK], v_sb[k][:, t, h, :],
                                probsT[:, h % TRING, t * TOK:(t + 1) * TOK], start=(t == 0), stop=(t == KT - 1),
                                tile_position=(0, 32 * j), skip_group_check=True)
                    mm.then_inc(pv_done, 1)

                def shared(name, bank):
                    mm = None
                    if name == "xT":
                        wait_turn(pe, x_in[1 - k], p, 1)
                        for c in range(DC):
                            mm = nc.tensor.transpose(bank[:, c * TOK:(c + 1) * TOK],
                                                     x_sb[1 - k][:, c * 128:(c + 1) * 128], ident[0:TOK, 0:TOK])
                    elif name == "Sc":
                        wait_step(pe, dve_pre, "xT", p)
                        for c in range(DC):
                            mm = nc.tensor.matmul(bank[0:TOK, 0:TOK], xT[:, c, :], xT[:, c, :],
                                                  start=(c == 0), stop=(c == DC - 1))
                    elif name in ("c0", "c1"):
                        c = int(name[1])
                        wait_turn(pe, ctx_in[1 - k], p, 1)
                        for j in range(KT):
                            mm = nc.tensor.transpose(bank[:, j * KP:(j + 1) * KP],
                                                     ctx_sb[1 - k][:, j, c * 128:(c + 1) * 128], ident[0:KP, 0:KP])
                    elif name == "PT":
                        wait_step(pe, dve_pre, "sparse", p)
                        mm = nc.tensor.transpose(bank[0:TOK, 0:TOK], sparse[:, :], ident[0:TOK, 0:TOK])
                    elif name == "att":
                        wait_step(pe, act_pre, "sparseT", p)
                        mm = nc.tensor.matmul(bank[0:TOK, 0:DIM], sparseT[:, :], x_sb[1 - k][:, :],
                                              start=True, stop=True)
                    elif name in ("K0", "K1"):
                        m = int(name[1])
                        wait_step(pe, act_pre, "c0", p)
                        wait_step(pe, dve_pre, "c1", p)
                        for c in range(DC):
                            mm = nc.tensor.matmul(bank[:, 0:KEYS], wk_sb[:, c, m * 128:(m + 1) * 128],
                                                  ctxT[:, c, :], start=(c == 0), stop=(c == DC - 1))
                    elif name == "x1T":
                        wait_step(pe, dve_pre, "x1", p)
                        for c in range(DC):
                            mm = nc.tensor.transpose(bank[:, c * TOK:(c + 1) * TOK],
                                                     x1[:, c * 128:(c + 1) * 128], ident[0:TOK, 0:TOK])
                    elif name == "qT":
                        wait_step(pe, act_pre, "x1T", p)
                        for m in range(DC):
                            for c in range(DC):
                                mm = nc.tensor.matmul(bank[:, m * TOK:(m + 1) * TOK],
                                                      wq_sb[:, c, m * 128:(m + 1) * 128], x1T[:, c, :],
                                                      start=(c == 0), stop=(c == DC - 1))
                    elif name in ("V0", "V1"):
                        for j in ((0, 1), (2,))[int(name[1])]:
                            for c in range(DC):
                                mm = nc.tensor.matmul(bank[0:KP, (j % 2) * DIM:(j % 2 + 1) * DIM],
                                                      ctxT[:, c, j * KP:(j + 1) * KP], wv_sb[:, c, :],
                                                      start=(c == 0), stop=(c == DC - 1))
                    elif name == "rb":
                        wait_step(pe, dve_post, "rden_wide", o)
                        for r in range(QUADS):
                            mm = nc.tensor.matmul(
                                bank[:, r * TOK:(r + 1) * TOK],
                                rden_wide[:, 4 * r:4 * r + 4, :].rearrange("q j d -> q (j d)"),
                                ident[0:TOK, 0:TOK], start=True, stop=True)
                    elif name == "Wo":
                        wait_step(pe, dve_post, "attnT", o)
                        for r in range(QUADS):
                            mm = nc.tensor.matmul(bank[0:TOK, 0:DIM], attnT[:, r * TOK:(r + 1) * TOK],
                                                  wo_sb[:, r, :], start=(r == 0), stop=(r == QUADS - 1))
                    elif name == "x2T":
                        wait_step(pe, dve_post, "x2", o)
                        for c in range(DC):
                            mm = nc.tensor.transpose(bank[:, c * TOK:(c + 1) * TOK],
                                                     x2[:, c * 128:(c + 1) * 128], ident[0:TOK, 0:TOK])
                    else:
                        wait_step(pe, dve_post, "x2_lo", o)
                        if name == "lg":
                            w_hi, w_lo, width = wr_hi[:, :, :], wr_lo[:, :, :], EXPERTS
                        else:
                            m, width = int(name[1]), 2 * DIM
                            w_hi = we_hi[:, :, m * width:(m + 1) * width]
                            w_lo = we_lo[:, :, m * width:(m + 1) * width]
                        parts = [(c, a, b) for c in range(DC)
                                 for a, b in ((x2_hi, w_hi), (x2_hi, w_lo), (x2_lo, w_hi))]
                        for n, (c, a, b) in enumerate(parts):
                            mm = nc.tensor.matmul(bank[0:TOK, 0:width], a[:, c, :], b[:, c, :],
                                                  start=(n == 0), stop=(n == len(parts) - 1))
                    return mm

                for n in range(SLOTS):
                    if attn and n < HEADS:
                        scores(n)
                    for u, (name, slot) in enumerate(USES):
                        if slot != n or not (post if name in POST_USES else pre):
                            continue
                        before = previous_use(u, it)
                        if before:
                            chain, step = taken[before[0]]
                            wait_step(pe, chain, step, shift(at, before[1]))
                        mm = shared(name, bank_of[name])
                        if name in POST_USES:
                            pe_post.did(name, mm)
                        else:
                            pe_pre.did(name, mm)
                    if attn and 2 <= n < HEADS + 2:
                        transpose_probs(n - 2)
                    if attn and n >= 6 and (n - 6) % 4 == 0:
                        weigh_values((n - 6) // 4)
                if it == -1:
                    expert_weights()
                    pe.wait_ge(we_split, 2 * EXPERTS)
                    pe.wait_ge(setup_dve, 8)

            run(pe, iteration)


_INS = [("x", "x"), ("ctx_1024", "context"), ("mask_Bx1xSxS2_bk1", "mask"), ("L0_attn_W", "attn_w"),
        ("L0_xattn_Wq", "wq"), ("L0_xattn_bq", "bq"), ("L0_xattn_Wk", "wk"), ("L0_xattn_bk", "bk"),
        ("L0_xattn_Wv", "wv"), ("L0_xattn_bv", "bv"), ("L0_xattn_Wo", "wo"), ("L0_xattn_bo", "bo"),
        ("L0_ffn_Wr", "wr"), ("L0_ffn_Wi", "wi"), ("L0_ffn_Wo", "wout")]


def kernel(**inputs):
    import numpy as np
    import concourse.bacc as bacc
    from concourse.bass_utils import run_bass_kernel_spmd

    nc = bacc.Bacc("TRN2", target_bir_lowering=False, num_devices=1)
    arrays, args = {}, {}
    for name, short in _INS:
        a = np.ascontiguousarray(inputs[name])
        if name.startswith("mask"):
            a = a.reshape(BATCH, TOK, KEYS)
        arrays[f"in_{short}"] = a
    consts = np.zeros((128, 128 + 2 + EXPERTS), np.float32)
    consts[:, 0:128] = np.eye(128, dtype=np.float32)
    for half in range(2):
        rows = np.arange(128) // HEAD_DIM % 2 == half
        consts[rows, 128 + half] = -Q_SCALE
    consts[:, 130:] = np.arange(EXPERTS, dtype=np.float32)
    arrays["in_consts"] = consts
    for key, a in arrays.items():
        args[key[3:]] = nc.dram_tensor(key, a.shape, mybir.dt.from_np(a.dtype), kind="ExternalInput").ap()
    out = nc.dram_tensor("out_dram", (BATCH, TOK, DIM), fp32, kind="ExternalOutput").ap()
    decoder_layer(nc, **args, out=out)
    r = run_bass_kernel_spmd(nc, [arrays], core_ids=[0])
    return r.results[0]["out_dram"]
```

```python
from contextlib import ExitStack

import concourse.bass as bass
from concourse import mybir

fp32, f32r, u8, u32 = mybir.dt.float32, mybir.dt.float32r, mybir.dt.uint8, mybir.dt.uint32
ALU = mybir.AluOpType
ACT = mybir.ActivationFunctionType
AX = mybir.AxisListType

BATCH, TOK, DIM, KEYS = 32, 112, 256, 375
HEADS, HEAD_DIM, EXPERTS = 16, 16, 8
KT = 3
KP = KEYS // KT
KEYS_EVEN = KEYS + KEYS % 2
DC = DIM // 128
PAIRS = 4
CHUNK_HEADS = 128 // HEAD_DIM
HEAD_ORDER = [CHUNK_HEADS * c + h for c in range(DC) for h in (0, 2, 4, 6, 1, 3, 5, 7)]
QUADS = HEADS // 4
SLOTS = HEADS + 4
BIG = 1e15
THRESH = 0.01
NEPS = 1e-5
SELF_SCALE = DIM ** -0.25
Q_SCALE = HEAD_DIM ** -0.5
RING = 4
TRING = 8
S_BANKS, T_BANKS, O_BANK, G_BANKS = (0, 1), (2, 3), 4, (5, 6, 7)

USES = [("m0", 0), ("x1T", 1), ("c0", 1), ("rb", 2), ("c1", 2), ("xT", 3), ("qT", 3), ("K0", 4),
        ("Wo", 5), ("Sc", 5), ("m1", 6), ("K1", 7), ("m2", 9), ("PT", 11), ("x2T", 11),
        ("att", 13), ("V0", 13), ("lg", 14), ("m3", 15), ("V1", 16)]
STAGES = {"self": (2, ("xT", "Sc", "PT", "att")),
          "proj": (1, ("x1T", "c0", "c1", "qT", "K0", "K1", "V0", "V1")),
          "attn": (0, ()),
          "join": (-1, ("rb", "Wo", "x2T", "lg")),
          "moe": (-2, ("m0", "m1", "m2", "m3"))}
STAGE_OF = {use: stage for stage, (_, uses) in STAGES.items() for use in uses}
FIRST, LAST = -2, BATCH + 1


class Chain:

    def __init__(self, sem, names):
        self.sem, self.names, self.at = sem, list(names), 0

    def did(self, name, instruction):
        assert self.names[self.at] == name, (self.names[self.at], name)
        self.at = (self.at + 1) % len(self.names)
        instruction.then_inc(self.sem, 1)


def count(at, per, k):
    t, c = at
    return per * c + k if isinstance(t, int) else 2 * per * t + (per * c + k)


def wait(eng, sem, at, per, k):
    v = count(at, per, k)
    if not isinstance(v, int) or v > 0:
        eng.wait_ge(sem, v)


def wait_step(eng, chain, name, at):
    wait(eng, chain.sem, at, len(chain.names), chain.names.index(name) + 1)


def wait_turn(eng, sem, at, per):
    t, c = at
    turns = c // 2 + 1
    if isinstance(t, int):
        if turns > 0:
            eng.wait_ge(sem, 16 * per * turns)
    else:
        eng.wait_ge(sem, 16 * per * t + 16 * per * turns)


def shift(at, by):
    return at[0], at[1] + by


def row(at):
    t, c = at
    return c if isinstance(t, int) else 2 * t + c


def active(stage, it):
    return 0 <= it + STAGES[stage][0] < BATCH


def previous_use(n, it):
    back, bank = 0, n % len(G_BANKS)
    m = n - 1
    while it + back >= FIRST:
        while m >= 0:
            name = USES[m][0]
            if m % len(G_BANKS) == bank and active(STAGE_OF[name], it + back):
                return name, back + STAGES[STAGE_OF[name]][0]
            m -= 1
        back -= 1
        m = len(USES) - 1
    return None


def decoder_layer(nc, x, context, mask, attn_w, wq, bq, wk, bk, wv, bv, wo, bo, wr, wi, wout,
                  consts, out):
    ctx = ExitStack()
    with ctx:
        def sb(name, shape, dt=fp32):
            return ctx.enter_context(nc.sbuf_tensor(name, shape, dt))

        def sem(name):
            return ctx.enter_context(nc.semaphore(name))

        const_sb = sb("const_sb", [128, 128 + 2 + EXPERTS])
        ident = const_sb[:, 0:128]
        head_masks = const_sb[:, 128:130]
        expert_ids = const_sb[0:TOK, 130:130 + EXPERTS]
        ones = sb("ones", [128, TOK])
        wq_sb = sb("wq_sb", [128, DC, DIM])
        wk_sb = sb("wk_sb", [128, DC, DIM])
        wv_sb = sb("wv_sb", [128, DC, DIM])
        wo_sb = sb("wo_sb", [128, DC, DIM])
        attn_w_sb = sb("attn_w_sb", [128, DC, DIM])
        attn_wT = sb("attn_wT", [128, DC, DIM])
        w_sum = sb("w_sum", [TOK, DIM])
        bq_col = sb("bq_col", [128, DC])
        bk_col = sb("bk_col", [128, DC])
        bv_row = sb("bv_row", [128, DIM])
        bo_row = sb("bo_row", [TOK, DIM])
        wr_sb = sb("wr_sb", [128, DC, EXPERTS])
        wr_hi = sb("wr_hi", [128, DC, EXPERTS], f32r)
        wr_lo = sb("wr_lo", [128, DC, EXPERTS], f32r)
        wi_sb = sb("wi_sb", [128, 2, DC, DIM])
        wout_sb = sb("wout_sb", [128, 2, DC, DIM])
        wiT = sb("wiT", [128, 2, DC, DIM])
        we_hi = sb("we_hi", [128, DC, EXPERTS * DIM], f32r)
        we_lo = sb("we_lo", [128, DC, EXPERTS * DIM], f32r)

        x_sb = [sb(f"x_sb{k}", [TOK, DIM]) for k in range(2)]
        ctx_sb = [sb(f"ctx_sb{k}", [KP, KT, DIM]) for k in range(2)]
        mask_u8 = [sb(f"mask_u8{k}", [TOK, KEYS], u8) for k in range(2)]
        mask_add = [sb(f"mask_add{k}", [TOK, KT, KP]) for k in range(2)]
        xT = sb("xT", [128, DC, TOK])
        self_nmax = sb("self_nmax", [TOK, 1])
        self_sum = sb("self_sum", [TOK, 1])
        self_rsum = sb("self_rsum", [TOK, 1])
        self_exp = sb("self_exp", [TOK, TOK])
        self_p = sb("self_p", [TOK, TOK])
        sparse = sb("sparse", [TOK, TOK])
        vacuum = sb("vacuum", [TOK, TOK])
        sparse_sum = sb("sparse_sum", [TOK, 1])
        sparse_den = sb("sparse_den", [TOK, 1])
        sparse_r = sb("sparse_r", [TOK, 1])
        vac_sum = sb("vac_sum", [TOK, 1])
        vac_scaled = sb("vac_scaled", [TOK, 1])
        x_cas = sb("x_cas", [TOK, DIM])
        sparseT = sb("sparseT", [TOK, TOK])
        y1 = sb("y1", [TOK, DIM])
        x1 = [sb(f"x1_{k}", [TOK, DIM]) for k in range(2)]
        x1_bo = [sb(f"x1_bo{k}", [TOK, DIM]) for k in range(2)]
        x1T = sb("x1T", [128, DC, TOK])
        ctxT = sb("ctxT", [128, DC, KEYS])
        k_hi = sb("k_hi", [128, DC, KEYS], f32r)
        k_lo = sb("k_lo", [128, DC, KEYS], f32r)
        q_sb = sb("q_sb", [128, DC, TOK])
        q_hi = sb("q_hi", [128, DC, 2, TOK], f32r)
        q_lo = sb("q_lo", [128, DC, 2, TOK], f32r)
        stats = [sb(f"stats{n}", [TOK, 6]) for n in range(3)]
        moments = [sb(f"moments{n}", [TOK, 2]) for n in range(3)]
        minus_half = sb("minus_half", [TOK, 1])
        var_eps = [sb(f"var_eps{n}", [TOK, 1]) for n in range(3)]
        rstd = [sb(f"rstd{n}", [TOK, 1]) for n in range(3)]

        k_stack = [sb(f"k_stack{k}", [96, DC, PAIRS, KEYS_EVEN], f32r) for k in range(2)]
        q_stack = [sb(f"q_stack{k}", [96, DC, PAIRS, 2, TOK], f32r) for k in range(2)]
        v_sb = [sb(f"v_sb{k}", [KP, KT, HEADS // 2, 3, HEAD_DIM]) for k in range(2)]
        masked = sb("masked", [TOK, RING, KEYS])
        nmax = sb("nmax", [TOK, HEADS])
        probs = sb("probs", [TOK, RING, KEYS])
        probs_sum = [sb(f"probs_sum{k}", [TOK, HEADS]) for k in range(2)]
        probsT = sb("probsT", [KP, TRING, KT * TOK])

        rden = sb("rden", [TOK, HEADS])
        rden_wide = sb("rden_wide", [TOK, HEADS, HEAD_DIM])
        o_sb = sb("o_sb", [128, DC * TOK])
        attnT = sb("attnT", [128, DC * TOK])
        y2 = sb("y2", [TOK, DIM])
        x2 = [sb(f"x2_{k}", [TOK, DIM]) for k in range(2)]
        x2_hi = [sb(f"x2_hi_{k}", [128, DC, TOK], f32r) for k in range(2)]
        x2_lo = [sb(f"x2_lo_{k}", [128, DC, TOK], f32r) for k in range(2)]
        gate_nmax = sb("gate_nmax", [TOK, 1])
        gate_sum = sb("gate_sum", [TOK, 1])
        gate_r = sb("gate_r", [TOK, 1])
        gate_exp = sb("gate_exp", [TOK, EXPERTS])
        gate_p = sb("gate_p", [TOK, EXPERTS])
        top_p = sb("top_p", [TOK, 8])
        top_i = sb("top_i", [TOK, 8], u32)
        top_f = sb("top_f", [TOK, 8])
        gate_a = sb("gate_a", [TOK, EXPERTS])
        gate_b = sb("gate_b", [TOK, EXPERTS])
        gate = [sb(f"gate_{k}", [TOK, EXPERTS]) for k in range(2)]
        mix = sb("mix", [TOK, DIM])
        out_sb = [sb(f"out_sb{k}", [TOK, DIM]) for k in range(2)]

        psum = ctx.enter_context(nc.psum_tensor("psum", [128, 8, 512], fp32))
        bank_of = {name: psum[:, G_BANKS[n % len(G_BANKS)], :] for n, (name, _) in enumerate(USES)}
        o_bank = psum[:, O_BANK, :]

        consts_in, attn_w_in, weights_in = sem("consts_in"), sem("attn_w_in"), sem("weights_in")
        WEIGHTS = 9
        wi_in = [sem("wi_in0"), sem("wi_in1")]
        x_in = [sem(f"x_in{k}") for k in range(2)]
        ctx_in = [sem(f"ctx_in{k}") for k in range(2)]
        mask_in = [sem(f"mask_in{k}") for k in range(2)]
        k_stacked = [sem(f"k_stacked{k}") for k in range(2)]
        q_stacked = [sem(f"q_stacked{k}") for k in range(2)]
        out_written = [sem(f"out_written{k}") for k in range(2)]
        setup_dve, setup_pe = sem("setup_dve"), sem("setup_pe")
        setup_pool, waits_passed = sem("setup_pool"), sem("waits_passed")
        wiT_ready, wiT_copied = sem("wiT_ready"), sem("wiT_copied")
        we_ready, we_split = sem("we_ready"), sem("we_split")
        scores_ready, masked_ready = sem("scores_ready"), sem("masked_ready")
        probs_ready, probsT_ready = sem("probs_ready"), sem("probsT_ready")
        probsT_copied, pv_done = sem("probsT_copied"), sem("pv_done")
        pe_steps = {stage: Chain(sem(f"pe_{stage}"), [u for u, _ in USES if STAGE_OF[u] == stage])
                    for stage in ("self", "proj", "join", "moe")}
        act_steps = {stage: Chain(sem(f"act_{stage}"), names) for stage, names in (
            ("self", ["self_exp", "sparseT"]),
            ("proj", ["x1T", "c0", "q0", "q1", "k_hi0", "k_hi1"]),
            ("join", ["o_sb", "x2_hi", "gate_exp"]))}
        dve_steps = {stage: Chain(sem(f"dve_{stage}"), names) for stage, names in (
            ("self", ["xT", "self_max", "self_rsum", "self_p", "sparse", "vacuum", "sparse_den",
                      "vac_scaled", "sparse_r", "x_cas", "y1", "stats1", "moments1", "x1"]),
            ("proj", ["c1", "q_hi0", "q_hi1", "k_lo0", "q_lo0", "q_lo1", "k_lo1", "v0", "v1", "v2"]),
            ("join", ["rden", "rden_wide", "attnT", "y2", "stats2", "moments2", "x2", "x2_lo", "gate_max",
                      "gate_r", "gate_p", "top_p", "top_i", "top_f", "gate_a", "gate_b", "gate"]),
            ("moe", [f"e{e}" for e in range(EXPERTS)] + ["stats3", "moments3", "out"]))}
        pool_steps = {stage: Chain(sem(f"pool_{stage}"), names) for stage, names in (
            ("self", ["var1", "rstd1"]), ("proj", ["mask", "x1_bo"]), ("join", ["var2", "rstd2"]),
            ("moe", ["var3", "rstd3"]))}
        taken = {"xT": (dve_steps, "xT"), "Sc": (act_steps, "self_exp"), "PT": (act_steps, "sparseT"),
                 "att": (dve_steps, "y1"), "x1T": (act_steps, "x1T"), "c0": (act_steps, "c0"),
                 "c1": (dve_steps, "c1"), "qT": (act_steps, "q1"), "K0": (dve_steps, "k_lo0"),
                 "K1": (dve_steps, "k_lo1"), "V0": (dve_steps, "v1"), "V1": (dve_steps, "v2"),
                 "rb": (dve_steps, "attnT"), "Wo": (dve_steps, "y2"), "x2T": (dve_steps, "x2_lo"),
                 "lg": (act_steps, "gate_exp"), "m0": (dve_steps, "e1"), "m1": (dve_steps, "e3"),
                 "m2": (dve_steps, "e5"), "m3": (dve_steps, "e7")}

        def settle(eng):
            eng.sem_inc(waits_passed, 1)

        def run(eng, iteration):
            head, tail = 4, BATCH - 4
            for it in range(FIRST, head):
                iteration((0, it), it)
            with eng.Fori(head // 2, tail // 2) as t:
                iteration((t, 0), head)
                iteration((t, 1), head + 1)
            for it in range(tail, LAST + 1):
                iteration((0, it), it)

        def stages(it):
            return [active(stage, it) for stage in STAGES]

        def batches(at):
            return *[shift(at, ahead) for ahead, _ in STAGES.values()], at[1] % 2

        block = ctx.enter_context(nc.Block())

        @block.sync
        def _(sp):
            def load_x(at):
                sp.dma_start(x_sb[at[1] % 2][:, :], x[row(at)]).then_inc(x_in[at[1] % 2], 16)

            def load_context(at):
                k = at[1] % 2
                sp.dma_start(ctx_sb[k][:, :, :], context[row(at)].rearrange("(p j) d -> p j d", j=KT))\
                  .then_inc(ctx_in[k], 16)
                sp.dma_start(mask_u8[k][:, :], mask[row(at)]).then_inc(mask_in[k], 16)

            def ready(chain, name, batch):
                wait_step(sp, chain, name, batch)
                settle(sp)

            sp.dma_start(const_sb[:, :], consts).then_inc(consts_in, 16)
            load_x((0, 0))
            sp.dma_start(attn_w_sb[:, :, :], attn_w.rearrange("(c p) n -> p c n", p=128)).then_inc(attn_w_in, 16)
            load_context((0, 0))
            for dst, src in ((wk_sb, wk), (wv_sb, wv), (wq_sb, wq), (wr_sb, wr), (wo_sb, wo)):
                sp.dma_start(dst[:, :, :], src.rearrange("(c p) n -> p c n", p=128)).then_inc(weights_in, 16)
            for dst, src in ((bq_col, bq), (bk_col, bk)):
                sp.dma_start(dst[:, :], src.rearrange("(c p) -> p c", p=128),
                             allow_slow_non_contiguous=True).then_inc(weights_in, 16)
            for dst, src in ((bv_row, bv), (bo_row, bo)):
                sp.dma_start(dst[:, :], src.rearrange("(a n) -> a n", a=1).broadcast_to([TOK if src is bo else 128, DIM]))\
                  .then_inc(weights_in, 16)

            def expert_weights():
                for e in range(EXPERTS):
                    if e >= 2:
                        sp.wait_ge(we_ready, e - 1)
                    sp.dma_start(wi_sb[:, e % 2, :, :], wi[e].rearrange("(c p) n -> p c n", p=128)).then_inc(wi_in[e % 2], 16)
                    sp.dma_start(wout_sb[:, e % 2, :, :], wout[e].rearrange("(c p) n -> p c n", p=128)).then_inc(wi_in[e % 2], 16)

            def iteration(at, it):
                own, proj, attn, join, moe = stages(it)
                s, p, a, o, m, k = batches(at)
                if active("self", it + 1):
                    ready(dve_steps["self"], "x1", p)
                    load_x(shift(at, 3))
                if active("proj", it + 1) and it > FIRST:
                    ready(pe_steps["proj"], "V1", a)
                    ready(pool_steps["proj"], "mask", a)
                    load_context(shift(at, 2))
                if proj:
                    wait(sp, scores_ready, o, HEADS, HEADS)
                    settle(sp)
                    ready(dve_steps["proj"], "q_lo1", p)
                    for g, part in enumerate((q_hi, q_hi, q_lo)):
                        for n in range(PAIRS):
                            sp.dma_start(q_stack[1 - k][32 * g:32 * g + 32, :, n, :, :].bitcast(fp32),
                                         part[32 * n:32 * n + 32, :, :, :].bitcast(fp32)).then_inc(q_stacked[1 - k], 16)
                    ready(act_steps["proj"], "k_hi1", p)
                    ready(dve_steps["proj"], "k_lo1", p)
                    for g, part in enumerate((k_hi, k_lo, k_hi)):
                        for n in range(PAIRS):
                            sp.dma_start(k_stack[1 - k][32 * g:32 * g + 32, :, n, 0:KEYS].bitcast(fp32),
                                         part[32 * n:32 * n + 32, :, :].bitcast(fp32)).then_inc(k_stacked[1 - k], 16)
                if moe:
                    ready(dve_steps["moe"], "out", m)
                    sp.dma_start(out[row(m)], out_sb[k][:, :]).then_inc(out_written[k], 16)
                if it == -1:
                    expert_weights()

            run(sp, iteration)
            for k in range(2):
                sp.wait_ge(out_written[k], 16 * BATCH // 2)

        @block.gpsimd
        def _(pool):
            nc.gpsimd.memset(minus_half[:, :], -0.5).then_inc(setup_pool, 1)
            pool.wait_ge(setup_pool, 1)
            pool.wait_ge(weights_in, 16 * WEIGHTS)

            def inverse_deviation(n, stage, batch):
                wait_step(pool, dve_steps[stage], f"moments{n}", batch)
                settle(pool)
                pool_steps[stage].did(f"var{n}", nc.gpsimd.tensor_scalar(
                    var_eps[n - 1][:, :], moments[n - 1][:, 1:2], NEPS, None, ALU.add))
                wait_step(pool, pool_steps[stage], f"var{n}", batch)
                pool_steps[stage].did(f"rstd{n}", nc.gpsimd.tensor_tensor(
                    rstd[n - 1][:, :], var_eps[n - 1][:, :], minus_half[:, :], ALU.pow))

            def iteration(at, it):
                own, proj, attn, join, moe = stages(it)
                s, p, a, o, m, k = batches(at)
                if proj:
                    wait_turn(pool, mask_in[1 - k], p, 1)
                    wait(pool, masked_ready, o, HEADS, HEADS)
                    settle(pool)
                    pool_steps["proj"].did("mask", nc.gpsimd.tensor_scalar(
                        mask_add[1 - k][:, :, :], mask_u8[1 - k][:, :].rearrange("t (p j) -> t j p", j=KT),
                        BIG, None, ALU.mult))
                if join:
                    inverse_deviation(2, "join", o)
                if proj:
                    wait_step(pool, dve_steps["self"], "x1", p)
                    wait_step(pool, dve_steps["join"], "y2", o)
                    pool_steps["proj"].did("x1_bo", nc.gpsimd.tensor_tensor(
                        x1_bo[1 - k][:, :], x1[1 - k][:, :], bo_row[:, :], ALU.add))
                if own:
                    inverse_deviation(1, "self", s)
                if moe:
                    inverse_deviation(3, "moe", m)

            run(pool, iteration)

        @block.scalar
        def _(act):
            own_steps, proj_steps, join_steps = (act_steps[stage] for stage in ("self", "proj", "join"))

            def iteration(at, it):
                own, proj, attn, join, moe = stages(it)
                s, p, a, o, m, k = batches(at)
                for n in range(SLOTS):
                    if join and n == 0:
                        wait(act, pv_done, o, QUADS, QUADS)
                        join_steps.did("o_sb", nc.scalar.activation(o_sb[:, :], o_bank[:, 0:DC * TOK], ACT.Copy))
                    if attn and n < HEADS:
                        h = HEAD_ORDER[n]
                        wait(act, masked_ready, a, HEADS, n + 1)
                        wait(act, probsT_ready, a, HEADS, n - RING + 1)
                        nc.scalar.activation(probs[:, n % RING, :], masked[:, n % RING, :], ACT.Exp,
                                             bias=nmax[:, n:n + 1], scale=-1.0,
                                             accum_out=probs_sum[k][:, h:h + 1]).then_inc(probs_ready, 1)
                    if attn and 3 <= n < HEADS + 3:
                        i = n - 3
                        wait(act, probsT_ready, a, HEADS, i + 1)
                        wait(act, pv_done, a, QUADS, i // 4 - 1)
                        nc.scalar.activation(probsT[:, i % TRING, :], psum[0:KP, T_BANKS[i % 2], 0:KT * TOK],
                                             ACT.Copy).then_inc(probsT_copied, 1)
                    if proj and n == 2:
                        if it == -1:
                            act.wait_ge(weights_in, 16 * WEIGHTS)
                        wait_step(act, pe_steps["proj"], "x1T", p)
                        proj_steps.did("x1T", nc.scalar.activation(
                            x1T[:, :, :].rearrange("p c t -> p (c t)"), bank_of["x1T"][:, 0:DC * TOK], ACT.Copy))
                        wait_step(act, pe_steps["proj"], "c0", p)
                        proj_steps.did("c0", nc.scalar.activation(ctxT[:, 0, :], bank_of["c0"][:, 0:KEYS], ACT.Copy))
                    if proj and n == 4:
                        wait_step(act, pe_steps["proj"], "qT", p)
                        for c in range(DC):
                            proj_steps.did(f"q{c}", nc.scalar.activation(
                                q_sb[:, c, :], bank_of["qT"][:, c * TOK:(c + 1) * TOK], ACT.Identity,
                                bias=bq_col[:, c:c + 1]))
                    if proj and n in (5, 8):
                        c = (n - 5) // 3
                        wait_step(act, pe_steps["proj"], f"K{c}", p)
                        if c == 0:
                            wait_turn(act, k_stacked[k], a, 12)
                        proj_steps.did(f"k_hi{c}", nc.scalar.activation(
                            k_hi[:, c, :], bank_of[f"K{c}"][:, 0:KEYS], ACT.Identity, bias=bk_col[:, c:c + 1]))
                    if own and n == 7:
                        wait_step(act, dve_steps["self"], "self_max", s)
                        own_steps.did("self_exp", nc.scalar.activation(
                            self_exp[:, :], bank_of["Sc"][0:TOK, 0:TOK], ACT.Exp, bias=self_nmax[:, :],
                            scale=1.0, accum_out=self_sum[:, :]))
                    if own and n == 12:
                        wait_step(act, pe_steps["self"], "PT", s)
                        own_steps.did("sparseT", nc.scalar.activation(
                            sparseT[:, :], bank_of["PT"][0:TOK, 0:TOK], ACT.Copy))
                    if join and n == 12:
                        wait_step(act, pe_steps["join"], "x2T", o)
                        join_steps.did("x2_hi", nc.scalar.activation(
                            x2_hi[1 - k][:, :, :].rearrange("p c t -> p (c t)"), bank_of["x2T"][:, 0:DC * TOK],
                            ACT.Copy))
                    if join and n == 16:
                        wait_step(act, dve_steps["join"], "gate_max", o)
                        join_steps.did("gate_exp", nc.scalar.activation(
                            gate_exp[:, :], bank_of["lg"][0:TOK, 0:EXPERTS], ACT.Exp, bias=gate_nmax[:, :],
                            scale=1.0, accum_out=gate_sum[:, :]))

            run(act, iteration)

        @block.vector
        def _(dve):
            for k in range(2):
                nc.vector.memset(v_sb[k][:, :, :, 1, :], 0.0)
                nc.vector.memset(k_stack[k][:, :, :, KEYS:KEYS_EVEN].bitcast(fp32), 0.0)
            nc.vector.memset(ones[:, :], 1.0).then_inc(setup_dve, 1)
            for c in range(DC):
                dve.wait_ge(setup_pe, c + 1)
                nc.vector.tensor_copy(attn_wT[:, c, :], psum[:, c, 0:DIM]).then_inc(setup_dve, 1)
            dve.wait_ge(setup_pe, DC + 1)
            nc.vector.tensor_copy(w_sum[:, :], psum[0:TOK, 2, 0:DIM]).then_inc(setup_dve, 1)

            def expert_weights():
                nc.vector.tensor_copy(wr_hi[:, :, :], wr_sb[:, :, :]).then_inc(setup_dve, 1)
                dve.wait_ge(setup_dve, 5)
                nc.vector.tensor_tensor(wr_lo[:, :, :], wr_sb[:, :, :], wr_hi[:, :, :].bitcast(fp32), ALU.subtract)\
                  .then_inc(setup_dve, 1)
                for e in range(EXPERTS):
                    dve.wait_ge(wiT_ready, e + 1)
                    nc.vector.tensor_copy(wiT[:, e % 2, :, :], psum[:, 0, :].rearrange("p (c n) -> p c n", c=DC))\
                      .then_inc(wiT_copied, 1)
                    dve.wait_ge(we_ready, e + 1)
                    prod = psum[:, 1 + e % 2, :].rearrange("p (c n) -> p c n", c=DC)
                    hi = we_hi[:, :, e * DIM:(e + 1) * DIM]
                    nc.vector.tensor_copy(hi, prod).then_inc(we_split, 1)
                    dve.wait_ge(we_split, 2 * e + 1)
                    nc.vector.tensor_tensor(we_lo[:, :, e * DIM:(e + 1) * DIM], prod, hi.bitcast(fp32), ALU.subtract)\
                      .then_inc(we_split, 1)

            own_steps, proj_steps, join_steps, moe_steps = (
                dve_steps[stage] for stage in ("self", "proj", "join", "moe"))

            def iteration(at, it):
                own, proj, attn, join, moe = stages(it)
                s, p, a, o, m, k = batches(at)

                def after(chain, name, batch):
                    wait_step(dve, chain, name, batch)

                def head(n):
                    wait(dve, scores_ready, a, HEADS, n + 1)
                    wait(dve, probs_ready, a, HEADS, n - RING + 1)
                    if n == 0:
                        after(pool_steps["proj"], "mask", a)
                    settle(dve)
                    nc.vector.tensor_tensor_reduce(
                        masked[:, n % RING, :], psum[0:TOK, S_BANKS[n % 2], 0:KEYS],
                        mask_add[k][:, :, :].rearrange("t j p -> t (j p)"), 1.0, 3.0e38, ALU.add, ALU.min,
                        nmax[:, n:n + 1]).then_inc(masked_ready, 1)

                def experts(n):
                    after(pe_steps["moe"], f"m{n}", m)
                    for e in (2 * n, 2 * n + 1):
                        if e:
                            after(moe_steps, f"e{e - 1}", m)
                        else:
                            after(join_steps, "gate", m)
                        moe_steps.did(f"e{e}", nc.vector.scalar_tensor_tensor(
                            out=mix[:, :], in0=bank_of[f"m{n}"][0:TOK, (e % 2) * DIM:(e % 2 + 1) * DIM],
                            scalar=gate[k][:, e:e + 1], in1=mix[:, :] if e else x2[k][:, :],
                            op0=ALU.mult, op1=ALU.add))

                def low_keys(c):
                    after(act_steps["proj"], f"k_hi{c}", p)
                    proj_steps.did(f"k_lo{c}", nc.vector.scalar_tensor_tensor(
                        out=k_lo[:, c, :], in0=bank_of[f"K{c}"][:, 0:KEYS], scalar=bk_col[:, c:c + 1],
                        in1=k_hi[:, c, :].bitcast(fp32), op0=ALU.add, op1=ALU.subtract))

                def values(tiles, use):
                    after(pe_steps["proj"], use, p)
                    for j in tiles:
                        proj_steps.did(f"v{j}", nc.vector.tensor_tensor(
                            v_sb[1 - k][:, j, :, 0:3:2, :],
                            bank_of[use][0:KP, (j % 2) * DIM:(j % 2 + 1) * DIM].rearrange(
                                "p (h e d) -> p h e d", e=2, d=HEAD_DIM),
                            bv_row[0:KP, :].rearrange("p (h e d) -> p h e d", e=2, d=HEAD_DIM), ALU.add))

                if join:
                    wait(dve, probs_ready, o, HEADS, HEADS)
                    join_steps.did("rden", nc.vector.reciprocal(rden[:, :], probs_sum[1 - k][:, :]))
                for n in range(SLOTS):
                    if attn and n < HEADS:
                        head(n)
                    if n == 0 and join:
                        after(join_steps, "rden", o)
                        join_steps.did("rden_wide", nc.vector.tensor_copy(
                            rden_wide[:, :, :], rden[:, :].unsqueeze(2).broadcast_to([TOK, HEADS, HEAD_DIM])))
                    if n == 1 and moe:
                        experts(0)
                    if n == 3:
                        if join:
                            after(pe_steps["join"], "rb", o)
                            after(act_steps["join"], "o_sb", o)
                            join_steps.did("attnT", nc.vector.tensor_tensor(
                                attnT[:, :], o_sb[:, :], bank_of["rb"][:, 0:DC * TOK], ALU.mult))
                        if proj:
                            after(pe_steps["proj"], "c1", p)
                            proj_steps.did("c1", nc.vector.tensor_copy(ctxT[:, 1, :], bank_of["c1"][:, 0:KEYS]))
                    if n == 4 and own:
                        after(pe_steps["self"], "xT", s)
                        own_steps.did("xT", nc.vector.tensor_scalar(
                            xT[:, :, :].rearrange("p c t -> p (c t)"), bank_of["xT"][:, 0:DC * TOK],
                            SELF_SCALE, None, ALU.mult))
                    if n == 5 and proj:
                        after(act_steps["proj"], "q1", p)
                        wait_turn(dve, q_stacked[k], a, 12)
                        for half in range(2):
                            proj_steps.did(f"q_hi{half}", nc.vector.tensor_scalar(
                                q_hi[:, :, half, :], q_sb[:, :, :], head_masks[:, half:half + 1], None, ALU.mult))
                    if n == 6:
                        if proj:
                            low_keys(0)
                            for half in range(2):
                                after(proj_steps, "q_hi1", p)
                                proj_steps.did(f"q_lo{half}", nc.vector.scalar_tensor_tensor(
                                    out=q_lo[:, :, half, :], in0=q_sb[:, :, :],
                                    scalar=head_masks[:, half:half + 1],
                                    in1=q_hi[:, :, half, :].bitcast(fp32), op0=ALU.mult, op1=ALU.subtract))
                        if join:
                            after(pe_steps["join"], "Wo", o)
                            after(pool_steps["proj"], "x1_bo", o)
                            join_steps.did("y2", nc.vector.tensor_tensor(
                                y2[:, :], bank_of["Wo"][0:TOK, 0:DIM], x1_bo[1 - k][:, :], ALU.add))
                        if own:
                            after(pe_steps["self"], "Sc", s)
                            own_steps.did("self_max", nc.vector.tensor_reduce(
                                self_nmax[:, :], bank_of["Sc"][0:TOK, 0:TOK], AX.X, ALU.max, negate=True))
                    if n == 7:
                        if join:
                            after(join_steps, "y2", o)
                            join_steps.did("stats2", nc.vector.bn_stats(stats[1][:, :], y2[:, :]))
                        if moe:
                            experts(1)
                    if n == 8:
                        if join:
                            after(join_steps, "stats2", o)
                            settle(dve)
                            join_steps.did("moments2", nc.vector.bn_aggr(moments[1][:, :], stats[1][:, :]))
                        if own:
                            after(act_steps["self"], "self_exp", s)
                            own_steps.did("self_rsum", nc.vector.reciprocal(self_rsum[:, :], self_sum[:, :]))
                    if n == 9:
                        if own:
                            after(own_steps, "self_rsum", s)
                            own_steps.did("self_p", nc.vector.tensor_scalar(
                                self_p[:, :], self_exp[:, :], self_rsum[:, :], None, ALU.mult))
                        if proj:
                            low_keys(1)
                        if join:
                            after(pool_steps["join"], "rstd2", o)
                            join_steps.did("x2", nc.vector.tensor_scalar(
                                x2[1 - k][:, :], y2[:, :], moments[1][:, 0:1], rstd[1][:, :],
                                ALU.subtract, ALU.mult))
                    if n == 10:
                        if own:
                            after(own_steps, "self_p", s)
                            own_steps.did("sparse", nc.vector.scalar_tensor_tensor(
                                out=sparse[:, :], in0=self_p[:, :], scalar=THRESH, in1=self_p[:, :],
                                op0=ALU.is_ge, op1=ALU.mult, accum_out=sparse_sum[:, :]))
                            own_steps.did("vacuum", nc.vector.scalar_tensor_tensor(
                                out=vacuum[:, :], in0=self_p[:, :], scalar=THRESH, in1=self_p[:, :],
                                op0=ALU.is_lt, op1=ALU.mult, accum_out=vac_sum[:, :]))
                        if moe:
                            experts(2)
                    if n == 11 and own:
                        after(own_steps, "vacuum", s)
                        own_steps.did("sparse_den", nc.vector.tensor_scalar(
                            sparse_den[:, :], sparse_sum[:, :], 1e-9, None, ALU.add))
                        own_steps.did("vac_scaled", nc.vector.tensor_scalar(
                            vac_scaled[:, :], vac_sum[:, :], 0.01, None, ALU.mult))
                    if n == 12 and own:
                        after(own_steps, "sparse_den", s)
                        own_steps.did("sparse_r", nc.vector.reciprocal(sparse_r[:, :], sparse_den[:, :]))
                        after(own_steps, "vac_scaled", s)
                        own_steps.did("x_cas", nc.vector.scalar_tensor_tensor(
                            out=x_cas[:, :], in0=w_sum[:, :], scalar=vac_scaled[:, :], in1=x_sb[k][:, :],
                            op0=ALU.mult, op1=ALU.add))
                    if n == 13 and join:
                        after(act_steps["join"], "x2_hi", o)
                        join_steps.did("x2_lo", nc.vector.tensor_tensor(
                            x2_lo[1 - k][:, :, :].rearrange("p c t -> p (c t)"), bank_of["x2T"][:, 0:DC * TOK],
                            x2_hi[1 - k][:, :, :].rearrange("p c t -> p (c t)").bitcast(fp32), ALU.subtract))
                    if n == 14:
                        if own:
                            after(pe_steps["self"], "att", s)
                            after(own_steps, "x_cas", s)
                            own_steps.did("y1", nc.vector.scalar_tensor_tensor(
                                out=y1[:, :], in0=bank_of["att"][0:TOK, 0:DIM], scalar=sparse_r[:, :],
                                in1=x_cas[:, :], op0=ALU.mult, op1=ALU.add))
                        if proj:
                            values((0, 1), "V0")
                    if n == 15:
                        if own:
                            after(own_steps, "y1", s)
                            own_steps.did("stats1", nc.vector.bn_stats(stats[0][:, :], y1[:, :]))
                        if join:
                            after(pe_steps["join"], "lg", o)
                            join_steps.did("gate_max", nc.vector.tensor_reduce(
                                gate_nmax[:, :], bank_of["lg"][0:TOK, 0:EXPERTS], AX.X, ALU.max, negate=True))
                    if n == 16:
                        if own:
                            after(own_steps, "stats1", s)
                            settle(dve)
                            own_steps.did("moments1", nc.vector.bn_aggr(moments[0][:, :], stats[0][:, :]))
                        if moe:
                            experts(3)
                        if join:
                            after(act_steps["join"], "gate_exp", o)
                            join_steps.did("gate_r", nc.vector.reciprocal(gate_r[:, :], gate_sum[:, :]))
                    if n == 17:
                        if moe:
                            after(moe_steps, f"e{EXPERTS - 1}", m)
                            moe_steps.did("stats3", nc.vector.bn_stats(stats[2][:, :], mix[:, :]))
                        if join:
                            after(join_steps, "gate_r", o)
                            join_steps.did("gate_p", nc.vector.tensor_scalar(
                                gate_p[:, :], gate_exp[:, :], gate_r[:, :], None, ALU.mult))
                        if moe:
                            after(moe_steps, "stats3", m)
                            settle(dve)
                            moe_steps.did("moments3", nc.vector.bn_aggr(moments[2][:, :], stats[2][:, :]))
                        if join:
                            after(join_steps, "gate_p", o)
                            settle(dve)
                            join_steps.did("top_p", nc.vector.max(top_p[:, :], gate_p[:, :]))
                        if own:
                            after(pool_steps["self"], "rstd1", s)
                            after(pool_steps["proj"], "x1_bo", a)
                            own_steps.did("x1", nc.vector.tensor_scalar(
                                x1[k][:, :], y1[:, :], moments[0][:, 0:1], rstd[0][:, :],
                                ALU.subtract, ALU.mult))
                    if n == 18:
                        if join:
                            after(join_steps, "top_p", o)
                            settle(dve)
                            join_steps.did("top_i", nc.vector.max_index(top_i[:, :], top_p[:, :], gate_p[:, :]))
                        if proj:
                            values((2,), "V1")
                        if join:
                            after(join_steps, "top_i", o)
                            join_steps.did("top_f", nc.vector.tensor_copy(top_f[:, :], top_i[:, :]))
                        if moe:
                            after(pool_steps["moe"], "rstd3", m)
                            wait_turn(dve, out_written[1 - k], shift(m, -1), 1)
                            moe_steps.did("out", nc.vector.tensor_scalar(
                                out_sb[k][:, :], mix[:, :], moments[2][:, 0:1], rstd[2][:, :],
                                ALU.subtract, ALU.mult))
                    if n == 19 and join:
                        after(join_steps, "top_f", o)
                        for which, dst in (("gate_a", gate_a), ("gate_b", gate_b)):
                            i = ("gate_a", "gate_b").index(which)
                            join_steps.did(which, nc.vector.tensor_scalar(
                                dst[:, :], expert_ids, top_f[:, i:i + 1], top_p[:, i:i + 1],
                                ALU.is_equal, ALU.mult))
                        after(join_steps, "gate_b", o)
                        join_steps.did("gate", nc.vector.tensor_tensor(
                            gate[1 - k][:, :], gate_a[:, :], gate_b[:, :], ALU.add))
                if it == -1:
                    expert_weights()

            run(dve, iteration)

        @block.tensor
        def _(pe):
            pe.wait_ge(consts_in, 16)
            pe.wait_ge(attn_w_in, 16)
            for c in range(DC):
                for r in range(DC):
                    mm = nc.tensor.transpose(psum[:, c, r * 128:(r + 1) * 128],
                                             attn_w_sb[:, r, c * 128:(c + 1) * 128], ident)
                mm.then_inc(setup_pe, 1)
            pe.wait_ge(setup_dve, 3)
            for c in range(DC):
                mm = nc.tensor.matmul(psum[0:TOK, 2, 0:DIM], ones[:, :], attn_wT[:, c, :],
                                      start=(c == 0), stop=(c == DC - 1))
            mm.then_inc(setup_pe, 1)

            def expert_weights():
                for e in range(EXPERTS):
                    pe.wait_ge(wi_in[e % 2], 32 * (e // 2 + 1))
                    if e:
                        pe.wait_ge(wiT_copied, e)
                    for c in range(DC):
                        for r in range(DC):
                            mm = nc.tensor.transpose(
                                psum[:, 0, c * DIM + r * 128:c * DIM + (r + 1) * 128],
                                wi_sb[:, e % 2, r, c * 128:(c + 1) * 128], ident)
                    mm.then_inc(wiT_ready, 1)
                    pe.wait_ge(wiT_copied, e + 1)
                    if e >= 2:
                        pe.wait_ge(we_split, 2 * (e - 1))
                    for r in range(DC):
                        for c in range(DC):
                            mm = nc.tensor.matmul(
                                psum[:, 1 + e % 2, r * DIM:(r + 1) * DIM],
                                wiT[:, e % 2, c, r * 128:(r + 1) * 128], wout_sb[:, e % 2, c, :],
                                start=(c == 0), stop=(c == DC - 1))
                    mm.then_inc(we_ready, 1)

            def iteration(at, it):
                own, proj, attn, join, moe = stages(it)
                s, p, a, o, m, k = batches(at)

                def scores(n):
                    if n == 0:
                        wait_turn(pe, q_stacked[k], a, 12)
                        wait_turn(pe, k_stacked[k], a, 12)
                    wait(pe, masked_ready, a, HEADS, n - 1)
                    c, pair, odd = HEAD_ORDER[n] // CHUNK_HEADS, HEAD_ORDER[n] % CHUNK_HEADS // 2, HEAD_ORDER[n] % 2
                    nc.tensor.matmul(psum[0:TOK, S_BANKS[n % 2], 0:KEYS_EVEN], q_stack[k][:, c, pair, odd, :],
                                     k_stack[k][:, c, pair, :], start=True, stop=True).then_inc(scores_ready, 1)

                def transpose_probs(n):
                    wait(pe, probs_ready, a, HEADS, n + 1)
                    wait(pe, probsT_copied, a, HEADS, n - 1)
                    for j in range(KT):
                        mm = nc.tensor.transpose(psum[0:KP, T_BANKS[n % 2], j * TOK:(j + 1) * TOK],
                                                 probs[:, n % RING, j * KP:(j + 1) * KP], ident[0:TOK, 0:TOK])
                    mm.then_inc(probsT_ready, 1)

                def weigh_values(quad):
                    c, odd = quad // 2, quad % 2
                    wait(pe, probsT_copied, a, HEADS, 4 * quad + 4)
                    if quad == 0:
                        wait_step(pe, dve_steps["proj"], "v2", a)
                        wait_step(pe, act_steps["join"], "o_sb", o)
                    for t in range(KT):
                        for j in range(4):
                            pair = 4 * c + j
                            mm = nc.tensor.matmul(
                                o_bank[32 * j:32 * j + 32, c * TOK:(c + 1) * TOK],
                                v_sb[k][:, t, pair, odd:odd + 2, :].rearrange("p e d -> p (e d)"),
                                probsT[:, (4 * quad + j) % TRING, t * TOK:(t + 1) * TOK],
                                start=(odd == 0 and t == 0), stop=(odd == 1 and t == KT - 1),
                                tile_position=(0, 32 * j), skip_group_check=True)
                    mm.then_inc(pv_done, 1)

                def product(name, bank):
                    mm = None
                    if name == "xT":
                        wait_turn(pe, x_in[k], s, 1)
                        for c in range(DC):
                            mm = nc.tensor.transpose(bank[:, c * TOK:(c + 1) * TOK],
                                                     x_sb[k][:, c * 128:(c + 1) * 128], ident[0:TOK, 0:TOK])
                    elif name == "Sc":
                        wait_step(pe, dve_steps["self"], "xT", s)
                        for c in range(DC):
                            mm = nc.tensor.matmul(bank[0:TOK, 0:TOK], xT[:, c, :], xT[:, c, :],
                                                  start=(c == 0), stop=(c == DC - 1))
                    elif name == "PT":
                        wait_step(pe, dve_steps["self"], "sparse", s)
                        mm = nc.tensor.transpose(bank[0:TOK, 0:TOK], sparse[:, :], ident[0:TOK, 0:TOK])
                    elif name == "att":
                        wait_step(pe, act_steps["self"], "sparseT", s)
                        mm = nc.tensor.matmul(bank[0:TOK, 0:DIM], sparseT[:, :], x_sb[k][:, :],
                                              start=True, stop=True)
                    elif name == "x1T":
                        wait_step(pe, dve_steps["self"], "x1", p)
                        for c in range(DC):
                            mm = nc.tensor.transpose(bank[:, c * TOK:(c + 1) * TOK],
                                                     x1[1 - k][:, c * 128:(c + 1) * 128], ident[0:TOK, 0:TOK])
                    elif name in ("c0", "c1"):
                        c = int(name[1])
                        wait_turn(pe, ctx_in[1 - k], p, 1)
                        for j in range(KT):
                            mm = nc.tensor.transpose(bank[:, j * KP:(j + 1) * KP],
                                                     ctx_sb[1 - k][:, j, c * 128:(c + 1) * 128], ident[0:KP, 0:KP])
                    elif name == "qT":
                        wait_step(pe, act_steps["proj"], "x1T", p)
                        for r in range(DC):
                            for c in range(DC):
                                mm = nc.tensor.matmul(bank[:, r * TOK:(r + 1) * TOK],
                                                      wq_sb[:, c, r * 128:(r + 1) * 128], x1T[:, c, :],
                                                      start=(c == 0), stop=(c == DC - 1))
                    elif name in ("K0", "K1"):
                        r = int(name[1])
                        wait_step(pe, act_steps["proj"], "c0", p)
                        wait_step(pe, dve_steps["proj"], "c1", p)
                        for c in range(DC):
                            mm = nc.tensor.matmul(bank[:, 0:KEYS], wk_sb[:, c, r * 128:(r + 1) * 128],
                                                  ctxT[:, c, :], start=(c == 0), stop=(c == DC - 1))
                    elif name in ("V0", "V1"):
                        for j in ((0, 1), (2,))[int(name[1])]:
                            for c in range(DC):
                                mm = nc.tensor.matmul(bank[0:KP, (j % 2) * DIM:(j % 2 + 1) * DIM],
                                                      ctxT[:, c, j * KP:(j + 1) * KP], wv_sb[:, c, :],
                                                      start=(c == 0), stop=(c == DC - 1))
                    elif name == "rb":
                        wait_step(pe, dve_steps["join"], "rden_wide", o)
                        for c in range(DC):
                            mm = nc.tensor.matmul(
                                bank[:, c * TOK:(c + 1) * TOK],
                                rden_wide[:, CHUNK_HEADS * c:CHUNK_HEADS * (c + 1), :].rearrange("q h d -> q (h d)"),
                                ident[0:TOK, 0:TOK], start=True, stop=True)
                    elif name == "Wo":
                        wait_step(pe, dve_steps["join"], "attnT", o)
                        for c in range(DC):
                            mm = nc.tensor.matmul(bank[0:TOK, 0:DIM], attnT[:, c * TOK:(c + 1) * TOK],
                                                  wo_sb[:, c, :], start=(c == 0), stop=(c == DC - 1))
                    elif name == "x2T":
                        wait_step(pe, dve_steps["join"], "x2", o)
                        for c in range(DC):
                            mm = nc.tensor.transpose(bank[:, c * TOK:(c + 1) * TOK],
                                                     x2[1 - k][:, c * 128:(c + 1) * 128], ident[0:TOK, 0:TOK])
                    else:
                        if name == "lg":
                            wait_step(pe, dve_steps["join"], "x2_lo", o)
                            hi, lo = x2_hi[1 - k], x2_lo[1 - k]
                            w_hi, w_lo, width = wr_hi[:, :, :], wr_lo[:, :, :], EXPERTS
                        else:
                            n, width, hi, lo = int(name[1]), 2 * DIM, x2_hi[k], x2_lo[k]
                            w_hi = we_hi[:, :, n * width:(n + 1) * width]
                            w_lo = we_lo[:, :, n * width:(n + 1) * width]
                        parts = [(c, x_part, w_part) for c in range(DC)
                                 for x_part, w_part in ((hi, w_hi), (hi, w_lo), (lo, w_hi))]
                        for n, (c, x_part, w_part) in enumerate(parts):
                            mm = nc.tensor.matmul(bank[0:TOK, 0:width], x_part[:, c, :], w_part[:, c, :],
                                                  start=(n == 0), stop=(n == len(parts) - 1))
                    return mm

                if attn:
                    scores(0)
                for n in range(SLOTS):
                    if attn and n + 1 < HEADS:
                        scores(n + 1)
                    for u, (name, slot) in enumerate(USES):
                        if slot != n or not active(STAGE_OF[name], it):
                            continue
                        before = previous_use(u, it)
                        if before:
                            steps, step = taken[before[0]]
                            wait_step(pe, steps[STAGE_OF[before[0]]], step, shift(at, before[1]))
                        pe_steps[STAGE_OF[name]].did(name, product(name, bank_of[name]))
                    if attn and 2 <= n < HEADS + 2:
                        transpose_probs(n - 2)
                    if attn and n >= 7 and (n - 7) % 4 == 0:
                        weigh_values((n - 7) // 4)
                if it == FIRST:
                    pe.wait_ge(weights_in, 16 * WEIGHTS)
                if it == -1:
                    expert_weights()
                    pe.wait_ge(we_split, 2 * EXPERTS)
                    pe.wait_ge(setup_dve, 6)

            run(pe, iteration)


_INS = [("x", "x"), ("ctx_1024", "context"), ("mask_Bx1xSxS2_bk1", "mask"), ("L0_attn_W", "attn_w"),
        ("L0_xattn_Wq", "wq"), ("L0_xattn_bq", "bq"), ("L0_xattn_Wk", "wk"), ("L0_xattn_bk", "bk"),
        ("L0_xattn_Wv", "wv"), ("L0_xattn_bv", "bv"), ("L0_xattn_Wo", "wo"), ("L0_xattn_bo", "bo"),
        ("L0_ffn_Wr", "wr"), ("L0_ffn_Wi", "wi"), ("L0_ffn_Wo", "wout")]


def kernel(**inputs):
    import numpy as np
    import concourse.bacc as bacc
    from concourse.bass_utils import run_bass_kernel_spmd

    nc = bacc.Bacc("TRN2", target_bir_lowering=False, num_devices=1)
    arrays, args = {}, {}
    for name, short in _INS:
        a = np.ascontiguousarray(inputs[name])
        if name.startswith("mask"):
            a = a.reshape(BATCH, TOK, KEYS)
        arrays[f"in_{short}"] = a
    consts = np.zeros((128, 128 + 2 + EXPERTS), np.float32)
    consts[:, 0:128] = np.eye(128, dtype=np.float32)
    for half in range(2):
        rows = np.arange(128) // HEAD_DIM % 2 == half
        consts[rows, 128 + half] = -Q_SCALE
    consts[:, 130:] = np.arange(EXPERTS, dtype=np.float32)
    arrays["in_consts"] = consts
    for key, a in arrays.items():
        args[key[3:]] = nc.dram_tensor(key, a.shape, mybir.dt.from_np(a.dtype), kind="ExternalInput").ap()
    out = nc.dram_tensor("out_dram", (BATCH, TOK, DIM), fp32, kind="ExternalOutput").ap()
    decoder_layer(nc, **args, out=out)
    r = run_bass_kernel_spmd(nc, [arrays], core_ids=[0])
    return r.results[0]["out_dram"]
```

```python
from contextlib import ExitStack

import concourse.bass as bass
from concourse import mybir

fp32, f32r, u8, u32 = mybir.dt.float32, mybir.dt.float32r, mybir.dt.uint8, mybir.dt.uint32
ALU = mybir.AluOpType
ACT = mybir.ActivationFunctionType
AX = mybir.AxisListType

BATCH, TOK, DIM, KEYS = 32, 112, 256, 375
HEADS, HEAD_DIM, EXPERTS = 16, 16, 8
KT = 3
KP = KEYS // KT
KEYS_EVEN = KEYS + KEYS % 2
DC = DIM // 128
PAIRS = 4
CHUNK_HEADS = 128 // HEAD_DIM
HEAD_ORDER = [CHUNK_HEADS * c + h for c in range(DC) for h in (0, 2, 4, 6, 1, 3, 5, 7)]
QUADS = HEADS // 4
SLOTS = HEADS + 4
BIG = 1e15
THRESH = 0.01
NEPS = 1e-5
SELF_SCALE = DIM ** -0.25
Q_SCALE = HEAD_DIM ** -0.5
RING = 4
TRING = 8
S_BANKS, T_BANKS, O_BANK, G_BANKS = (0, 1), (2, 3), 4, (5, 6, 7)

USES = [("x1T", 0, "G1"), ("c0", 0, "G2"), ("c1", 0, "G0"), ("m0", 1, "G1"), ("rb", 1, "O"),
        ("xT", 2, "G0"), ("qT", 2, "G2"), ("K0", 3, "G0"), ("Wo", 4, "G1"), ("Sc", 5, "G2"),
        ("K1", 6, "G1"), ("m1", 8, "G0"), ("V0", 9, "G2"), ("x2T", 10, "G1"), ("PT", 11, "G0"),
        ("m2", 12, "G2"), ("att", 13, "G1"), ("lg", 14, "G0"), ("V1", 15, "G2"), ("m3", 16, "G1"),
        ("V2", 18, "G0")]
WEIGHT_USES = [("T0", 1, "G1"), ("E0", 3, "G1"), ("T1", 7, "G0"), ("T2", 8, "G2"), ("E1", 9, "G0"),
               ("E2", 10, "G1"), ("T3", 12, "G2"), ("E3", 14, "G0")]
STAGES = {"self": (2, ("xT", "Sc", "PT", "att")),
          "proj": (1, ("x1T", "c0", "c1", "qT", "K0", "K1", "V0", "V1", "V2")),
          "attn": (0, ()),
          "join": (-1, ("rb", "Wo", "x2T", "lg")),
          "moe": (-2, ("m0", "m1", "m2", "m3")),
          "weights": (1, tuple(use for use, _, _ in WEIGHT_USES))}
EXPERTS_PER = 4
STAGE_OF = {use: stage for stage, (_, uses) in STAGES.items() for use in uses}
ALL_USES = sorted(USES + WEIGHT_USES, key=lambda use: use[1])
FIRST, LAST = -2, BATCH + 2


class Chain:

    def __init__(self, sem, names):
        self.sem, self.names, self.at = sem, list(names), 0

    def did(self, name):
        assert self.names[self.at] == name, (self.names[self.at], name)
        self.at = (self.at + 1) % len(self.names)
        return self.sem

    def to(self, name, at):
        return count(at, len(self.names), self.names.index(name) + 1)


def count(at, per, k):
    t, c = at
    return per * c + k if isinstance(t, int) else 2 * per * t + (per * c + k)


def turn(at, per):
    t, c = at
    turns = 16 * per * (c // 2 + 1)
    return turns if isinstance(t, int) else 16 * per * t + turns


def due(value):
    return not isinstance(value, int) or value > 0


def shift(at, by):
    return at[0], at[1] + by


def row(at):
    t, c = at
    return c if isinstance(t, int) else 2 * t + c


def active(stage, it):
    if stage == "weights":
        return 0 <= it + 1 < EXPERTS // EXPERTS_PER
    return 0 <= it + STAGES[stage][0] < BATCH


def previous_use(n, it):
    back, m, bank = 0, n - 1, ALL_USES[n][2]
    while it + back >= FIRST:
        while m >= 0:
            name = ALL_USES[m][0]
            if ALL_USES[m][2] == bank and active(STAGE_OF[name], it + back):
                return name, back + STAGES[STAGE_OF[name]][0]
            m -= 1
        back -= 1
        m = len(ALL_USES) - 1
    return None


def decoder_layer(nc, x, context, mask, attn_w, wq, bq, wk, bk, wv, bv, wo, bo, wr, wi, wout,
                  consts, out):
    ctx = ExitStack()
    with ctx:
        def sb(name, shape, dt=fp32):
            return ctx.enter_context(nc.sbuf_tensor(name, shape, dt))

        def sem(name):
            return ctx.enter_context(nc.semaphore(name))

        const_sb = sb("const_sb", [128, 128 + 2 + EXPERTS])
        ident = const_sb[:, 0:128]
        head_masks = const_sb[:, 128:130]
        expert_ids = const_sb[0:TOK, 130:130 + EXPERTS]
        ones = sb("ones", [128, TOK])
        wq_sb = sb("wq_sb", [128, DC, DIM])
        wk_hi, wk_lo = sb("wk_hi", [128, DC, DIM], f32r), sb("wk_lo", [128, DC, DIM], f32r)
        wv_hi, wv_lo = sb("wv_hi", [128, DC, DIM], f32r), sb("wv_lo", [128, DC, DIM], f32r)
        wo_sb = sb("wo_sb", [128, DC, DIM])
        w_sum = sb("w_sum", [TOK, DIM])
        bq_col = sb("bq_col", [128, DC])
        bk_col = sb("bk_col", [128, DC])
        bv_row = sb("bv_row", [128, DIM])
        bo_row = sb("bo_row", [TOK, DIM])
        wr_sb = sb("wr_sb", [128, DC, EXPERTS])
        wr_hi = sb("wr_hi", [128, DC, EXPERTS], f32r)
        wr_lo = sb("wr_lo", [128, DC, EXPERTS], f32r)
        wi_sb = sb("wi_sb", [128, EXPERTS, DC, DIM])
        wout_sb = sb("wout_sb", [128, EXPERTS, DC, DIM])
        wiT = sb("wiT", [128, 2, DC, DIM])
        wk_sb, wv_sb = wiT[:, 0, :, :], wiT[:, 1, :, :]
        we_hi = sb("we_hi", [128, DC, EXPERTS * DIM], f32r)
        we_lo = sb("we_lo", [128, DC, EXPERTS * DIM], f32r)

        x_sb = [sb(f"x_sb{k}", [TOK, DIM]) for k in range(2)]
        ctx_sb = [sb(f"ctx_sb{k}", [KP, KT, DIM]) for k in range(2)]
        mask_u8 = [sb(f"mask_u8{k}", [TOK, KEYS], u8) for k in range(2)]
        mask_add = [sb(f"mask_add{k}", [TOK, KT, KP]) for k in range(2)]
        xT = sb("xT", [128, DC, TOK])
        self_nmax = sb("self_nmax", [TOK, 1])
        self_sum = sb("self_sum", [TOK, 1])
        self_rsum = sb("self_rsum", [TOK, 1])
        self_exp = sb("self_exp", [TOK, TOK])
        self_p = sb("self_p", [TOK, TOK])
        sparse = sb("sparse", [TOK, TOK])
        vacuum = sb("vacuum", [TOK, TOK])
        sparse_sum = sb("sparse_sum", [TOK, 1])
        sparse_den = sb("sparse_den", [TOK, 1])
        sparse_r = sb("sparse_r", [TOK, 1])
        vac_sum = sb("vac_sum", [TOK, 1])
        vac_scaled = sb("vac_scaled", [TOK, 1])
        x_cas = sb("x_cas", [TOK, DIM])
        sparseT = sb("sparseT", [TOK, TOK])
        y1 = sb("y1", [TOK, DIM])
        x1 = [sb(f"x1_{k}", [TOK, DIM]) for k in range(2)]
        x1_bo = [sb(f"x1_bo{k}", [TOK, DIM]) for k in range(2)]
        x1T = sb("x1T", [128, DC, TOK])
        ctx_hi = sb("ctx_hi", [128, DC, KEYS_EVEN], f32r)
        ctx_lo = sb("ctx_lo", [128, DC, KEYS_EVEN], f32r)
        k_hi = sb("k_hi", [128, DC, KEYS], f32r)
        k_lo = sb("k_lo", [128, DC, KEYS], f32r)
        attn_w_sb = k_hi[:, :, 0:DIM].bitcast(fp32)
        attn_wT = k_lo[:, :, 0:DIM].bitcast(fp32)
        q_sb = sb("q_sb", [128, DC, TOK])
        q_hi = sb("q_hi", [128, DC, 2, TOK], f32r)
        q_lo = sb("q_lo", [128, DC, 2, TOK], f32r)
        stats = [sb(f"stats{n}", [TOK, 6]) for n in range(3)]
        moments = [sb(f"moments{n}", [TOK, 2]) for n in range(3)]
        minus_half = sb("minus_half", [TOK, 1])
        var_eps = [sb(f"var_eps{n}", [TOK, 1]) for n in range(3)]
        rstd = [sb(f"rstd{n}", [TOK, 1]) for n in range(3)]

        k_stack = [sb(f"k_stack{k}", [96, DC, PAIRS, KEYS_EVEN], f32r) for k in range(2)]
        q_stack = [sb(f"q_stack{k}", [96, DC, PAIRS, 2, TOK], f32r) for k in range(2)]
        v_sb = [sb(f"v_sb{k}", [KP, KT, HEADS // 2, 3, HEAD_DIM]) for k in range(2)]
        masked = sb("masked", [TOK, RING, KEYS])
        nmax = sb("nmax", [TOK, HEADS])
        probs = sb("probs", [TOK, RING, KEYS])
        probs_sum = [sb(f"probs_sum{k}", [TOK, HEADS]) for k in range(2)]
        probsT = sb("probsT", [KP, TRING, KT * TOK])

        rden = sb("rden", [TOK, HEADS])
        rden_wide = sb("rden_wide", [TOK, HEADS, HEAD_DIM])
        o_sb = sb("o_sb", [128, DC * TOK])
        attnT = sb("attnT", [128, DC * TOK])
        y2 = sb("y2", [TOK, DIM])
        x2 = [sb(f"x2_{k}", [TOK, DIM]) for k in range(2)]
        x2_hi = [sb(f"x2_hi_{k}", [128, DC, TOK], f32r) for k in range(2)]
        x2_lo = [sb(f"x2_lo_{k}", [128, DC, TOK], f32r) for k in range(2)]
        gate_nmax = sb("gate_nmax", [TOK, 1])
        gate_sum = sb("gate_sum", [TOK, 1])
        gate_r = sb("gate_r", [TOK, 1])
        gate_exp = sb("gate_exp", [TOK, EXPERTS])
        gate_p = sb("gate_p", [TOK, EXPERTS])
        top_p = sb("top_p", [TOK, 8])
        top_i = sb("top_i", [TOK, 8], u32)
        top_f = sb("top_f", [TOK, 8])
        gate_a = sb("gate_a", [TOK, EXPERTS])
        gate_b = sb("gate_b", [TOK, EXPERTS])
        gate = [sb(f"gate_{k}", [TOK, EXPERTS]) for k in range(2)]
        mix = sb("mix", [TOK, DIM])
        out_sb = [sb(f"out_sb{k}", [TOK, DIM]) for k in range(2)]

        psum = ctx.enter_context(nc.psum_tensor("psum", [128, 8, 512], fp32))
        shared = dict(zip(("G0", "G1", "G2", "O"), G_BANKS + (O_BANK,)))
        bank_of = {name: psum[:, shared[bank], :] for name, _, bank in ALL_USES}
        o_bank = psum[:, O_BANK, :]

        consts_in, attn_w_in, weights_in = sem("consts_in"), sem("attn_w_in"), sem("weights_in")
        WEIGHTS = 9
        wi_in = [sem("wi_in0"), sem("wi_in1")]
        x_in = [sem(f"x_in{k}") for k in range(2)]
        ctx_in = [sem(f"ctx_in{k}") for k in range(2)]
        mask_in = [sem(f"mask_in{k}") for k in range(2)]
        k_stacked = [[sem(f"k_stacked{k}_{pair}") for pair in range(PAIRS)] for k in range(2)]
        q_stacked = [[sem(f"q_stacked{k}_{pair}") for pair in range(PAIRS)] for k in range(2)]
        out_written = [sem(f"out_written{k}") for k in range(2)]
        setup_dve, setup_pe = sem("setup_dve"), sem("setup_pe")
        setup_pool, waits_passed = sem("setup_pool"), sem("waits_passed")
        scores_ready, masked_ready = sem("scores_ready"), sem("masked_ready")
        probs_ready, probsT_ready = sem("probs_ready"), sem("probsT_ready")
        probsT_copied, pv_done = sem("probsT_copied"), sem("pv_done")
        pe_steps = {stage: Chain(sem(f"pe_{stage}"), [u for u, _, _ in ALL_USES if STAGE_OF[u] == stage])
                    for stage in ("self", "proj", "join", "moe", "weights")}
        act_steps = {stage: Chain(sem(f"act_{stage}"), names) for stage, names in (
            ("self", ["xT", "self_exp", "sparseT"]),
            ("proj", ["x1T", "ctx_hi0", "ctx_hi1", "q0", "q1", "k_hi0", "k_hi1"]),
            ("join", ["o_sb", "x2_hi", "gate_exp"]),
            ("weights", [f"wiT{u[1]}" if u[0] == "T" else f"we_hi{u[1]}" for u, _, _ in WEIGHT_USES]))}
        dve_steps = {stage: Chain(sem(f"dve_{stage}"), names) for stage, names in (
            ("self", ["self_max", "self_rsum", "self_p", "sparse", "vacuum", "sparse_den",
                      "vac_scaled", "sparse_r", "x_cas", "y1", "stats1", "moments1", "x1"]),
            ("proj", ["ctx_lo0", "ctx_lo1", "q_hi0", "q_hi1", "q_lo0", "q_lo1", "k_lo0", "k_lo1", "v0", "v1", "v2"]),
            ("attn", ["rden", "rden_wide"]),
            ("join", ["attnT", "y2", "stats2", "moments2", "x2", "x2_lo", "gate_max",
                      "gate_r", "gate_p", "top_p", "top_i", "top_f", "gate_a", "gate_b", "gate"]),
            ("moe", [f"e{e}" for e in range(EXPERTS)] + ["stats3", "moments3", "out"]),
            ("weights", [f"we_lo{j}" for j in range(EXPERTS_PER)]))}
        pool_steps = {stage: Chain(sem(f"pool_{stage}"), names) for stage, names in (
            ("self", ["var1", "rstd1"]), ("proj", ["mask", "x1_bo"]), ("join", ["var2", "rstd2"]),
            ("moe", ["var3", "rstd3"]))}
        pe_self, pe_proj, pe_join, pe_moe, pe_weights = pe_steps.values()
        act_self, act_proj, act_join, act_weights = act_steps.values()
        dve_self, dve_proj, dve_attn, dve_join, dve_moe, dve_weights = dve_steps.values()
        pool_self, pool_proj, pool_join, pool_moe = pool_steps.values()
        taken = {"xT": (act_steps, "xT"), "Sc": (act_steps, "self_exp"), "PT": (act_steps, "sparseT"),
                 "att": (dve_steps, "y1"), "x1T": (act_steps, "x1T"), "c0": (dve_steps, "ctx_lo0"),
                 "c1": (dve_steps, "ctx_lo1"), "qT": (act_steps, "q1"), "K0": (dve_steps, "k_lo0"),
                 "K1": (dve_steps, "k_lo1"), "V0": (dve_steps, "v0"), "V1": (dve_steps, "v1"), "V2": (dve_steps, "v2"),
                 "rb": (dve_steps, "attnT"), "Wo": (dve_steps, "y2"), "x2T": (dve_steps, "x2_lo"),
                 "lg": (act_steps, "gate_exp"), "m0": (dve_steps, "e1"), "m1": (dve_steps, "e3"),
                 "m2": (dve_steps, "e5"), "m3": (dve_steps, "e7")}
        for j in range(EXPERTS_PER):
            taken[f"T{j}"], taken[f"E{j}"] = (act_steps, f"wiT{j}"), (dve_steps, f"we_lo{j}")

        def settle(eng):
            eng.sem_inc(waits_passed, 1)

        def run(eng, iteration):
            head, tail = 4, BATCH - 4
            for it in range(FIRST, head):
                iteration((0, it), it)
            with eng.Fori(head // 2, tail // 2) as t:
                iteration((t, 0), head)
                iteration((t, 1), head + 1)
            for it in range(tail, LAST + 1):
                iteration((0, it), it)

        def stages(it):
            return [active(stage, it) for stage in ("self", "proj", "attn", "join", "moe")]

        def batches(at):
            return *[shift(at, ahead) for ahead in (2, 1, 0, -1, -2)], at[1] % 2

        block = ctx.enter_context(nc.Block())

        @block.sync
        def _(sp):
            def load_x(at):
                sp.dma_start(x_sb[at[1] % 2][:, :], x[row(at)]).then_inc(x_in[at[1] % 2], 16)

            def load_context(at):
                k = at[1] % 2
                sp.dma_start(ctx_sb[k][:, :, :], context[row(at)].rearrange("(p j) d -> p j d", j=KT))\
                  .then_inc(ctx_in[k], 16)
                sp.dma_start(mask_u8[k][:, :], mask[row(at)]).then_inc(mask_in[k], 16)

            sp.dma_start(const_sb[:, :], consts).then_inc(consts_in, 16)
            load_x((0, 0))
            sp.dma_start(attn_w_sb[:, :, :], attn_w.rearrange("(c p) n -> p c n", p=128))\
              .then_inc(attn_w_in, 16)
            load_context((0, 0))
            for dst, src in ((wk_sb, wk), (wv_sb, wv), (wq_sb, wq), (wr_sb, wr), (wo_sb, wo)):
                sp.dma_start(dst[:, :, :], src.rearrange("(c p) n -> p c n", p=128))\
                  .then_inc(weights_in, 16)
            for dst, src in ((bq_col, bq), (bk_col, bk)):
                sp.dma_start(dst[:, :], src.rearrange("(c p) -> p c", p=128),
                             allow_slow_non_contiguous=True).then_inc(weights_in, 16)
            for dst, src in ((bv_row, bv), (bo_row, bo)):
                sp.dma_start(dst[:, :], src.rearrange("(a n) -> a n", a=1).broadcast_to([TOK if src is bo else 128, DIM]))\
                  .then_inc(weights_in, 16)

            def expert_weights():
                for part in range(EXPERTS // EXPERTS_PER):
                    e = slice(part * EXPERTS_PER, (part + 1) * EXPERTS_PER)
                    for dst, src in ((wi_sb, wi), (wout_sb, wout)):
                        sp.dma_start(dst[:, e, :, :], src[e].rearrange("e (c p) n -> p e c n", p=128))\
                          .then_inc(wi_in[part], 16)

            def iteration(at, it):
                own, proj, attn, join, moe = stages(it)
                s, p, a, o, m, k = batches(at)
                if active("self", it + 1):
                    if due(dve_self.to("x1", p)):
                        sp.wait_ge(dve_self.sem, dve_self.to("x1", p))
                    settle(sp)
                    load_x(shift(at, 3))
                if active("proj", it + 1) and it > FIRST:
                    if due(pe_proj.to("c1", a)):
                        sp.wait_ge(pe_proj.sem, pe_proj.to("c1", a))
                    settle(sp)
                    if due(pool_proj.to("mask", a)):
                        sp.wait_ge(pool_proj.sem, pool_proj.to("mask", a))
                    settle(sp)
                    load_context(shift(at, 2))
                if active("moe", it - 1):
                    sp.wait_ge(dve_moe.sem, dve_moe.to("out", shift(m, -1)))
                    settle(sp)
                    sp.dma_start(out[row(shift(m, -1))], out_sb[1 - k][:, :]).then_inc(out_written[1 - k], 16)
                if proj:
                    if due(count(o, HEADS, HEADS)):
                        sp.wait_ge(scores_ready, count(o, HEADS, HEADS))
                    settle(sp)
                    sp.wait_ge(dve_proj.sem, dve_proj.to("q_lo1", p))
                    settle(sp)
                    for n in range(PAIRS):
                        for g, part in enumerate((q_hi, q_hi, q_lo)):
                            sp.dma_start(q_stack[1 - k][32 * g:32 * g + 32, :, n, :, :].bitcast(fp32),
                                         part[32 * n:32 * n + 32, :, :, :].bitcast(fp32))\
                                           .then_inc(q_stacked[1 - k][n], 16)
                    sp.wait_ge(act_proj.sem, act_proj.to("k_hi1", p))
                    settle(sp)
                    sp.wait_ge(dve_proj.sem, dve_proj.to("k_lo1", p))
                    settle(sp)
                    for n in range(PAIRS):
                        for g, part in enumerate((k_hi, k_lo, k_hi)):
                            sp.dma_start(k_stack[1 - k][32 * g:32 * g + 32, :, n, 0:KEYS].bitcast(fp32),
                                         part[32 * n:32 * n + 32, :, :].bitcast(fp32))\
                                           .then_inc(k_stacked[1 - k][n], 16)
                if it == FIRST:
                    expert_weights()

            run(sp, iteration)
            for k in range(2):
                sp.wait_ge(out_written[k], 16 * BATCH // 2)

        @block.gpsimd
        def _(pool):
            nc.gpsimd.memset(minus_half[:, :], -0.5).then_inc(setup_pool, 1)
            pool.wait_ge(setup_pool, 1)
            pool.wait_ge(weights_in, 16 * WEIGHTS)

            def inverse_deviation(n, stage, batch):
                pool.wait_ge(dve_steps[stage].sem, dve_steps[stage].to(f"moments{n}", batch))
                settle(pool)
                nc.gpsimd.tensor_scalar(
                    var_eps[n - 1][:, :], moments[n - 1][:, 1:2], NEPS, None, ALU.add)\
                      .then_inc(pool_steps[stage].did(f"var{n}"), 1)
                pool.wait_ge(pool_steps[stage].sem, pool_steps[stage].to(f"var{n}", batch))
                nc.gpsimd.tensor_tensor(
                    rstd[n - 1][:, :], var_eps[n - 1][:, :], minus_half[:, :], ALU.pow)\
                      .then_inc(pool_steps[stage].did(f"rstd{n}"), 1)

            def iteration(at, it):
                own, proj, attn, join, moe = stages(it)
                s, p, a, o, m, k = batches(at)
                if proj:
                    pool.wait_ge(mask_in[1 - k], turn(p, 1))
                    if due(count(o, HEADS, HEADS)):
                        pool.wait_ge(masked_ready, count(o, HEADS, HEADS))
                    settle(pool)
                    nc.gpsimd.tensor_scalar(
                        mask_add[1 - k][:, :, :], mask_u8[1 - k][:, :].rearrange("t (p j) -> t j p", j=KT),
                        BIG, None, ALU.mult).then_inc(pool_proj.did("mask"), 1)
                if join:
                    inverse_deviation(2, "join", o)
                if proj:
                    pool.wait_ge(dve_self.sem, dve_self.to("x1", p))
                    if due(dve_join.to("y2", o)):
                        pool.wait_ge(dve_join.sem, dve_join.to("y2", o))
                    nc.gpsimd.tensor_tensor(
                        x1_bo[1 - k][:, :], x1[1 - k][:, :], bo_row[:, :], ALU.add)\
                          .then_inc(pool_proj.did("x1_bo"), 1)
                if own:
                    inverse_deviation(1, "self", s)
                if moe:
                    inverse_deviation(3, "moe", m)

            run(pool, iteration)

        @block.scalar
        def _(act):

            def iteration(at, it):
                own, proj, attn, join, moe = stages(it)
                s, p, a, o, m, k = batches(at)

                def exponent(a, n):
                    h = HEAD_ORDER[n]
                    act.wait_ge(masked_ready, count(a, HEADS, n + 1))
                    if due(count(a, HEADS, n - RING + 1)):
                        act.wait_ge(probsT_ready, count(a, HEADS, n - RING + 1))
                    nc.scalar.activation(probs[:, n % RING, :], masked[:, n % RING, :], ACT.Exp,
                                         bias=nmax[:, n:n + 1], scale=-1.0,
                                         accum_out=probs_sum[a[1] % 2][:, h:h + 1]).then_inc(probs_ready, 1)

                for n in range(SLOTS):
                    if proj and n == 0:
                        if it == -1:
                            act.wait_ge(weights_in, 16 * WEIGHTS)
                        act.wait_ge(pe_proj.sem, pe_proj.to("x1T", p))
                        nc.scalar.activation(
                            x1T[:, :, :].rearrange("p c t -> p (c t)"), bank_of["x1T"][:, 0:DC * TOK], ACT.Copy)\
                              .then_inc(act_proj.did("x1T"), 1)
                    if join and n == 0:
                        act.wait_ge(pv_done, count(o, QUADS, QUADS))
                        nc.scalar.activation(o_sb[:, :], o_bank[:, 0:DC * TOK], ACT.Copy)\
                          .then_inc(act_join.did("o_sb"), 1)
                    if proj and n == 0:
                        for c in range(DC):
                            act.wait_ge(pe_proj.sem, pe_proj.to(f"c{c}", p))
                            nc.scalar.activation(
                                ctx_hi[:, c, 0:KEYS], bank_of[f"c{c}"][:, 0:KEYS], ACT.Copy)\
                                  .then_inc(act_proj.did(f"ctx_hi{c}"), 1)
                    if attn and 3 <= n < HEADS + 3:
                        i = n - 3
                        act.wait_ge(probsT_ready, count(a, HEADS, i + 1))
                        if due(count(a, QUADS, i // 4 - 1)):
                            act.wait_ge(pv_done, count(a, QUADS, i // 4 - 1))
                        nc.scalar.activation(probsT[:, i % TRING, :], psum[0:KP, T_BANKS[i % 2], 0:KT * TOK],
                                             ACT.Copy).then_inc(probsT_copied, 1)
                    if own and n == 2:
                        act.wait_ge(pe_self.sem, pe_self.to("xT", s))
                        nc.scalar.activation(
                            xT[:, :, :].rearrange("p c t -> p (c t)"), bank_of["xT"][:, 0:DC * TOK],
                            ACT.Copy, scale=SELF_SCALE).then_inc(act_self.did("xT"), 1)
                    if attn and 0 < n < HEADS:
                        exponent(a, n)
                    if n == SLOTS - 1 and active("attn", it + 1):
                        exponent(p, 0)
                    if proj and n == 3:
                        act.wait_ge(pe_proj.sem, pe_proj.to("qT", p))
                        for c in range(DC):
                            nc.scalar.activation(
                                q_sb[:, c, :], bank_of["qT"][:, c * TOK:(c + 1) * TOK], ACT.Identity,
                                bias=bq_col[:, c:c + 1]).then_inc(act_proj.did(f"q{c}"), 1)
                    if own and n == 6:
                        act.wait_ge(dve_self.sem, dve_self.to("self_max", s))
                        nc.scalar.activation(
                            self_exp[:, :], bank_of["Sc"][0:TOK, 0:TOK], ACT.Exp, bias=self_nmax[:, :],
                            scale=1.0, accum_out=self_sum[:, :]).then_inc(act_self.did("self_exp"), 1)
                    if proj and n in (4, 7):
                        c = (n - 4) // 3
                        act.wait_ge(pe_proj.sem, pe_proj.to(f"K{c}", p))
                        if c == 0 and attn:
                            act.wait_ge(scores_ready, count(a, HEADS, PAIRS))
                        nc.scalar.activation(
                            k_hi[:, c, :], bank_of[f"K{c}"][:, 0:KEYS], ACT.Identity, bias=bk_col[:, c:c + 1])\
                              .then_inc(act_proj.did(f"k_hi{c}"), 1)
                    if own and n == 12:
                        act.wait_ge(pe_self.sem, pe_self.to("PT", s))
                        nc.scalar.activation(
                            sparseT[:, :], bank_of["PT"][0:TOK, 0:TOK], ACT.Copy)\
                              .then_inc(act_self.did("sparseT"), 1)
                    if join and n == 10:
                        act.wait_ge(pe_join.sem, pe_join.to("x2T", o))
                        nc.scalar.activation(
                            x2_hi[1 - k][:, :, :].rearrange("p c t -> p (c t)"), bank_of["x2T"][:, 0:DC * TOK],
                            ACT.Copy).then_inc(act_join.did("x2_hi"), 1)
                    if join and n == 16:
                        act.wait_ge(dve_join.sem, dve_join.to("gate_max", o))
                        nc.scalar.activation(
                            gate_exp[:, :], bank_of["lg"][0:TOK, 0:EXPERTS], ACT.Exp, bias=gate_nmax[:, :],
                            scale=1.0, accum_out=gate_sum[:, :]).then_inc(act_join.did("gate_exp"), 1)
                    for name, slot, _ in WEIGHT_USES:
                        if active("weights", it) and name[0] == "T" and slot + 1 == n:
                            act.wait_ge(pe_weights.sem, pe_weights.to(name, p))
                            nc.scalar.activation(
                                wiT[:, int(name[1]) % 2, :, :].rearrange("p c n -> p (c n)"), bank_of[name],
                                ACT.Copy).then_inc(act_weights.did(f"wiT{name[1]}"), 1)
                        if active("weights", it) and name[0] == "E" and slot + 1 == n:
                            e = EXPERTS_PER * p[1] + int(name[1])
                            act.wait_ge(pe_weights.sem, pe_weights.to(name, p))
                            nc.scalar.activation(
                                we_hi[:, :, e * DIM:(e + 1) * DIM],
                                bank_of[name].rearrange("p (c n) -> p c n", c=DC),
                                ACT.Copy).then_inc(act_weights.did(f"we_hi{name[1]}"), 1)

            run(act, iteration)

        @block.vector
        def _(dve):
            for k in range(2):
                nc.vector.memset(v_sb[k][:, :, :, 1, :], 0.0)
                nc.vector.memset(k_stack[k][:, :, :, KEYS:KEYS_EVEN].bitcast(fp32), 0.0)
            for part in (ctx_hi, ctx_lo):
                nc.vector.memset(part[:, :, KEYS:KEYS_EVEN].bitcast(fp32), 0.0)
            nc.vector.memset(ones[:, :], 1.0).then_inc(setup_dve, 1)
            def split_weights(weights, done):
                for src, hi, lo in weights:
                    nc.vector.tensor_copy(hi[:, :, :], src[:, :, :]).then_inc(setup_dve, 1)
                for n, (src, hi, lo) in enumerate(weights):
                    dve.wait_ge(setup_dve, done + n + 1)
                    nc.vector.tensor_tensor(lo[:, :, :], src[:, :, :], hi[:, :, :].bitcast(fp32), ALU.subtract)\
                      .then_inc(setup_dve, 1)

            def low_product(j, w):
                dve.wait_ge(act_weights.sem, act_weights.to(f"we_hi{j}", w))
                e = EXPERTS_PER * w[1] + j
                nc.vector.tensor_tensor(
                    we_lo[:, :, e * DIM:(e + 1) * DIM], bank_of[f"E{j}"].rearrange("p (c n) -> p c n", c=DC),
                    we_hi[:, :, e * DIM:(e + 1) * DIM].bitcast(fp32), ALU.subtract)\
                  .then_inc(dve_weights.did(f"we_lo{j}"), 1)

            def iteration(at, it):
                own, proj, attn, join, moe = stages(it)
                s, p, a, o, m, k = batches(at)

                def head(a, n):
                    dve.wait_ge(scores_ready, count(a, HEADS, n + 1))
                    if due(count(a, HEADS, n - RING + 1)):
                        dve.wait_ge(probs_ready, count(a, HEADS, n - RING + 1))
                    if n == 0:
                        dve.wait_ge(pool_proj.sem, pool_proj.to("mask", a))
                    settle(dve)
                    k = a[1] % 2
                    nc.vector.tensor_tensor_reduce(
                        masked[:, n % RING, :], psum[0:TOK, S_BANKS[n % 2], 0:KEYS],
                        mask_add[k][:, :, :].rearrange("t j p -> t (j p)"), 1.0, 3.0e38, ALU.add, ALU.min,
                        nmax[:, n:n + 1]).then_inc(masked_ready, 1)

                def expert(e):
                    dve.wait_ge(pe_moe.sem, pe_moe.to(f"m{e // 2}", m))
                    if e:
                        dve.wait_ge(dve_moe.sem, dve_moe.to(f"e{e - 1}", m))
                    else:
                        dve.wait_ge(dve_join.sem, dve_join.to("gate", m))
                        if due(dve_moe.to("out", shift(m, -1))):
                            dve.wait_ge(dve_moe.sem, dve_moe.to("out", shift(m, -1)))
                    nc.vector.scalar_tensor_tensor(
                        out=mix[:, :], in0=bank_of[f"m{e // 2}"][0:TOK, (e % 2) * DIM:(e % 2 + 1) * DIM],
                        scalar=gate[k][:, e:e + 1], in1=mix[:, :] if e else x2[k][:, :],
                        op0=ALU.mult, op1=ALU.add).then_inc(dve_moe.did(f"e{e}"), 1)

                def low_keys(c):
                    dve.wait_ge(act_proj.sem, act_proj.to(f"k_hi{c}", p))
                    nc.vector.scalar_tensor_tensor(
                        out=k_lo[:, c, :], in0=bank_of[f"K{c}"][:, 0:KEYS], scalar=bk_col[:, c:c + 1],
                        in1=k_hi[:, c, :].bitcast(fp32), op0=ALU.add, op1=ALU.subtract)\
                          .then_inc(dve_proj.did(f"k_lo{c}"), 1)

                def values(j):
                    dve.wait_ge(pe_proj.sem, pe_proj.to(f"V{j}", p))
                    nc.vector.tensor_tensor(
                        v_sb[1 - k][:, j, :, 0:3:2, :],
                        bank_of[f"V{j}"][0:KP, 0:DIM].rearrange("p (h e d) -> p h e d", e=2, d=HEAD_DIM),
                        bv_row[0:KP, :].rearrange("p (h e d) -> p h e d", e=2, d=HEAD_DIM), ALU.add)\
                          .then_inc(dve_proj.did(f"v{j}"), 1)

                for n in range(SLOTS):
                    if it == FIRST and n == 10:
                        for c in range(DC):
                            dve.wait_ge(setup_pe, c + 1)
                            nc.vector.tensor_copy(attn_wT[:, c, :], psum[:, c, 0:DIM]).then_inc(setup_dve, 1)
                    if it == FIRST and n == 13:
                        dve.wait_ge(setup_pe, DC + 1)
                        nc.vector.tensor_copy(w_sum[:, :], psum[0:TOK, 2, 0:DIM]).then_inc(setup_dve, 1)
                    if attn and 1 < n < HEADS:
                        head(a, n)
                    if n == 1 and proj:
                        for c in range(DC):
                            dve.wait_ge(act_proj.sem, act_proj.to(f"ctx_hi{c}", p))
                            nc.vector.tensor_tensor(
                                ctx_lo[:, c, 0:KEYS], bank_of[f"c{c}"][:, 0:KEYS],
                                ctx_hi[:, c, 0:KEYS].bitcast(fp32), ALU.subtract)\
                                  .then_inc(dve_proj.did(f"ctx_lo{c}"), 1)
                    if n == 1 and active("moe", it - 1):
                        dve.wait_ge(pool_moe.sem, pool_moe.to("rstd3", shift(m, -1)))
                        if due(turn(shift(m, -2), 1)):
                            dve.wait_ge(out_written[k], turn(shift(m, -2), 1))
                        nc.vector.tensor_scalar(
                            out_sb[1 - k][:, :], mix[:, :], moments[2][:, 0:1], rstd[2][:, :],
                            ALU.subtract, ALU.mult).then_inc(dve_moe.did("out"), 1)
                    if n == 2 and join:
                        dve.wait_ge(pe_join.sem, pe_join.to("rb", o))
                        dve.wait_ge(act_join.sem, act_join.to("o_sb", o))
                        nc.vector.tensor_tensor(
                            attnT[:, :], o_sb[:, :], bank_of["rb"][:, 0:DC * TOK], ALU.mult)\
                              .then_inc(dve_join.did("attnT"), 1)
                    if n == 3 and moe:
                        expert(0)
                        expert(1)
                    if n == 4 and proj:
                        dve.wait_ge(act_proj.sem, act_proj.to("q1", p))
                        if attn:
                            dve.wait_ge(scores_ready, count(a, HEADS, PAIRS))
                        for half in range(2):
                            nc.vector.tensor_scalar(
                                q_hi[:, :, half, :], q_sb[:, :, :], head_masks[:, half:half + 1], None, ALU.mult)\
                                  .then_inc(dve_proj.did(f"q_hi{half}"), 1)
                    if n == 5 and proj:
                        for half in range(2):
                            dve.wait_ge(dve_proj.sem, dve_proj.to("q_hi1", p))
                            nc.vector.scalar_tensor_tensor(
                                out=q_lo[:, :, half, :], in0=q_sb[:, :, :],
                                scalar=head_masks[:, half:half + 1],
                                in1=q_hi[:, :, half, :].bitcast(fp32), op0=ALU.mult, op1=ALU.subtract)\
                                  .then_inc(dve_proj.did(f"q_lo{half}"), 1)
                    if n == 5:
                        if join:
                            dve.wait_ge(pe_join.sem, pe_join.to("Wo", o))
                            dve.wait_ge(pool_proj.sem, pool_proj.to("x1_bo", o))
                            nc.vector.tensor_tensor(
                                y2[:, :], bank_of["Wo"][0:TOK, 0:DIM], x1_bo[1 - k][:, :], ALU.add)\
                                  .then_inc(dve_join.did("y2"), 1)
                    if n == 6:
                        if join:
                            dve.wait_ge(dve_join.sem, dve_join.to("y2", o))
                            nc.vector.bn_stats(stats[1][:, :], y2[:, :]).then_inc(dve_join.did("stats2"), 1)
                        if own:
                            dve.wait_ge(pe_self.sem, pe_self.to("Sc", s))
                            nc.vector.tensor_reduce(
                                self_nmax[:, :], bank_of["Sc"][0:TOK, 0:TOK], AX.X, ALU.max, negate=True)\
                                  .then_inc(dve_self.did("self_max"), 1)
                        if proj:
                            low_keys(0)
                    if n == 7:
                        if join:
                            dve.wait_ge(dve_join.sem, dve_join.to("stats2", o))
                            settle(dve)
                            nc.vector.bn_aggr(moments[1][:, :], stats[1][:, :])\
                              .then_inc(dve_join.did("moments2"), 1)
                    if n == 8:
                        if own:
                            dve.wait_ge(act_self.sem, act_self.to("self_exp", s))
                            nc.vector.reciprocal(self_rsum[:, :], self_sum[:, :])\
                              .then_inc(dve_self.did("self_rsum"), 1)
                            dve.wait_ge(dve_self.sem, dve_self.to("self_rsum", s))
                            nc.vector.tensor_scalar(
                                self_p[:, :], self_exp[:, :], self_rsum[:, :], None, ALU.mult)\
                                  .then_inc(dve_self.did("self_p"), 1)
                    if n == 9:
                        if join:
                            dve.wait_ge(pool_join.sem, pool_join.to("rstd2", o))
                            nc.vector.tensor_scalar(
                                x2[1 - k][:, :], y2[:, :], moments[1][:, 0:1], rstd[1][:, :],
                                ALU.subtract, ALU.mult).then_inc(dve_join.did("x2"), 1)
                        if own:
                            dve.wait_ge(dve_self.sem, dve_self.to("self_p", s))
                            nc.vector.scalar_tensor_tensor(
                                out=sparse[:, :], in0=self_p[:, :], scalar=THRESH, in1=self_p[:, :],
                                op0=ALU.is_ge, op1=ALU.mult, accum_out=sparse_sum[:, :])\
                                  .then_inc(dve_self.did("sparse"), 1)
                            nc.vector.scalar_tensor_tensor(
                                out=vacuum[:, :], in0=self_p[:, :], scalar=THRESH, in1=self_p[:, :],
                                op0=ALU.is_lt, op1=ALU.mult, accum_out=vac_sum[:, :])\
                                  .then_inc(dve_self.did("vacuum"), 1)
                        if proj:
                            low_keys(1)
                    if n == 10 and moe:
                        expert(2)
                        expert(3)
                    if n == 11 and proj:
                        values(0)
                    if n == 11 and own:
                        dve.wait_ge(dve_self.sem, dve_self.to("vacuum", s))
                        nc.vector.tensor_scalar(
                            sparse_den[:, :], sparse_sum[:, :], 1e-9, None, ALU.add)\
                              .then_inc(dve_self.did("sparse_den"), 1)
                        nc.vector.tensor_scalar(
                            vac_scaled[:, :], vac_sum[:, :], 0.01, None, ALU.mult)\
                              .then_inc(dve_self.did("vac_scaled"), 1)
                    if n == 12:
                        if join:
                            dve.wait_ge(act_join.sem, act_join.to("x2_hi", o))
                            nc.vector.tensor_tensor(
                                x2_lo[1 - k][:, :, :].rearrange("p c t -> p (c t)"), bank_of["x2T"][:, 0:DC * TOK],
                                x2_hi[1 - k][:, :, :].rearrange("p c t -> p (c t)").bitcast(fp32), ALU.subtract)\
                                  .then_inc(dve_join.did("x2_lo"), 1)
                    if n == 13:
                        if own:
                            dve.wait_ge(dve_self.sem, dve_self.to("sparse_den", s))
                            nc.vector.reciprocal(sparse_r[:, :], sparse_den[:, :])\
                              .then_inc(dve_self.did("sparse_r"), 1)
                            if it == FIRST:
                                dve.wait_ge(setup_dve, DC + 2)
                            dve.wait_ge(dve_self.sem, dve_self.to("vac_scaled", s))
                            nc.vector.scalar_tensor_tensor(
                                out=x_cas[:, :], in0=w_sum[:, :], scalar=vac_scaled[:, :], in1=x_sb[k][:, :],
                                op0=ALU.mult, op1=ALU.add).then_inc(dve_self.did("x_cas"), 1)
                    if n == 14 and moe:
                        expert(4)
                        expert(5)
                    if n == 15 and own:
                        dve.wait_ge(pe_self.sem, pe_self.to("att", s))
                        dve.wait_ge(dve_self.sem, dve_self.to("x_cas", s))
                        nc.vector.scalar_tensor_tensor(
                            out=y1[:, :], in0=bank_of["att"][0:TOK, 0:DIM], scalar=sparse_r[:, :],
                            in1=x_cas[:, :], op0=ALU.mult, op1=ALU.add).then_inc(dve_self.did("y1"), 1)
                    if n == 15:
                        if own:
                            dve.wait_ge(dve_self.sem, dve_self.to("y1", s))
                            nc.vector.bn_stats(stats[0][:, :], y1[:, :]).then_inc(dve_self.did("stats1"), 1)
                        if join:
                            dve.wait_ge(pe_join.sem, pe_join.to("lg", o))
                            nc.vector.tensor_reduce(
                                gate_nmax[:, :], bank_of["lg"][0:TOK, 0:EXPERTS], AX.X, ALU.max, negate=True)\
                                  .then_inc(dve_join.did("gate_max"), 1)
                    if n == 16:
                        if own:
                            dve.wait_ge(dve_self.sem, dve_self.to("stats1", s))
                            settle(dve)
                            nc.vector.bn_aggr(moments[0][:, :], stats[0][:, :])\
                              .then_inc(dve_self.did("moments1"), 1)
                        if proj:
                            values(1)
                    if n == 17:
                        if join:
                            dve.wait_ge(act_join.sem, act_join.to("gate_exp", o))
                            nc.vector.reciprocal(gate_r[:, :], gate_sum[:, :])\
                              .then_inc(dve_join.did("gate_r"), 1)
                        if attn:
                            dve.wait_ge(probs_ready, count(a, HEADS, HEADS))
                            nc.vector.reciprocal(rden[:, :], probs_sum[k][:, :])\
                              .then_inc(dve_attn.did("rden"), 1)
                        if join:
                            dve.wait_ge(dve_join.sem, dve_join.to("gate_r", o))
                            nc.vector.tensor_scalar(
                                gate_p[:, :], gate_exp[:, :], gate_r[:, :], None, ALU.mult)\
                                  .then_inc(dve_join.did("gate_p"), 1)
                        if own:
                            dve.wait_ge(pool_self.sem, pool_self.to("rstd1", s))
                            if due(pool_proj.to("x1_bo", a)):
                                dve.wait_ge(pool_proj.sem, pool_proj.to("x1_bo", a))
                            nc.vector.tensor_scalar(
                                x1[k][:, :], y1[:, :], moments[0][:, 0:1], rstd[0][:, :],
                                ALU.subtract, ALU.mult).then_inc(dve_self.did("x1"), 1)
                    if n == 18:
                        if join:
                            dve.wait_ge(dve_join.sem, dve_join.to("gate_p", o))
                            settle(dve)
                            nc.vector.max(top_p[:, :], gate_p[:, :]).then_inc(dve_join.did("top_p"), 1)
                        if attn:
                            dve.wait_ge(dve_attn.sem, dve_attn.to("rden", a))
                            if it > 0:
                                dve.wait_ge(pe_join.sem, pe_join.to("rb", o))
                            nc.vector.tensor_copy(
                                rden_wide[:, :, :], rden[:, :].unsqueeze(2).broadcast_to([TOK, HEADS, HEAD_DIM]))\
                              .then_inc(dve_attn.did("rden_wide"), 1)
                        if join:
                            dve.wait_ge(dve_join.sem, dve_join.to("top_p", o))
                            settle(dve)
                            nc.vector.max_index(top_i[:, :], top_p[:, :], gate_p[:, :])\
                              .then_inc(dve_join.did("top_i"), 1)
                        if moe:
                            expert(EXPERTS - 2)
                        if join:
                            dve.wait_ge(dve_join.sem, dve_join.to("top_i", o))
                            nc.vector.tensor_copy(top_f[:, :], top_i[:, :])\
                              .then_inc(dve_join.did("top_f"), 1)
                        if moe:
                            expert(EXPERTS - 1)
                        if active("attn", it + 1):
                            head(p, 0)
                        if join:
                            dve.wait_ge(dve_join.sem, dve_join.to("top_f", o))
                            nc.vector.tensor_scalar(
                                gate_a[:, :], expert_ids, top_f[:, 0:1], top_p[:, 0:1],
                                ALU.is_equal, ALU.mult).then_inc(dve_join.did("gate_a"), 1)
                            nc.vector.tensor_scalar(
                                gate_b[:, :], expert_ids, top_f[:, 1:2], top_p[:, 1:2],
                                ALU.is_equal, ALU.mult).then_inc(dve_join.did("gate_b"), 1)
                        if proj:
                            values(2)
                        if moe:
                            dve.wait_ge(dve_moe.sem, dve_moe.to(f"e{EXPERTS - 1}", m))
                            nc.vector.bn_stats(stats[2][:, :], mix[:, :]).then_inc(dve_moe.did("stats3"), 1)
                        if join:
                            dve.wait_ge(dve_join.sem, dve_join.to("gate_b", o))
                            nc.vector.tensor_tensor(
                                gate[1 - k][:, :], gate_a[:, :], gate_b[:, :], ALU.add)\
                              .then_inc(dve_join.did("gate"), 1)
                        if moe:
                            dve.wait_ge(dve_moe.sem, dve_moe.to("stats3", m))
                            settle(dve)
                            nc.vector.bn_aggr(moments[2][:, :], stats[2][:, :])\
                              .then_inc(dve_moe.did("moments3"), 1)
                    if n == SLOTS - 1:
                        if active("attn", it + 1):
                            head(p, 1)
                    for name, slot, _ in WEIGHT_USES:
                        if active("weights", it) and name[0] == "E" and min(slot + 2, SLOTS - 1) == n:
                            low_product(int(name[1]), p)
                if it == FIRST:
                    dve.wait_ge(weights_in, 16 * WEIGHTS)
                    split_weights(((wk_sb, wk_hi, wk_lo), (wv_sb, wv_hi, wv_lo)), 4)
                if it == -1:
                    split_weights(((wr_sb, wr_hi, wr_lo),), 8)

            run(dve, iteration)

        @block.tensor
        def _(pe):
            pe.wait_ge(consts_in, 16)

            def transpose_attn_w():
                pe.wait_ge(attn_w_in, 16)
                for c in range(DC):
                    for r in range(DC):
                        mm = nc.tensor.transpose(psum[:, c, r * 128:(r + 1) * 128],
                                                 attn_w_sb[:, r, c * 128:(c + 1) * 128], ident)
                    mm.then_inc(setup_pe, 1)

            def sum_attn_w():
                pe.wait_ge(setup_dve, DC + 1)
                for c in range(DC):
                    mm = nc.tensor.matmul(psum[0:TOK, 2, 0:DIM], ones[:, :], attn_wT[:, c, :],
                                          start=(c == 0), stop=(c == DC - 1))
                mm.then_inc(setup_pe, 1)

            def iteration(at, it):
                own, proj, attn, join, moe = stages(it)
                s, p, a, o, m, k = batches(at)

                def scores(a, n):
                    k = a[1] % 2
                    if n < PAIRS:
                        pe.wait_ge(q_stacked[k][n], turn(a, 3))
                        pe.wait_ge(k_stacked[k][n], turn(a, 3))
                    if due(count(a, HEADS, n - 1)):
                        pe.wait_ge(masked_ready, count(a, HEADS, n - 1))
                    c, pair, odd = HEAD_ORDER[n] // CHUNK_HEADS, HEAD_ORDER[n] % CHUNK_HEADS // 2, HEAD_ORDER[n] % 2
                    nc.tensor.matmul(psum[0:TOK, S_BANKS[n % 2], 0:KEYS_EVEN], q_stack[k][:, c, pair, odd, :],
                                     k_stack[k][:, c, pair, :], start=True, stop=True)\
                                       .then_inc(scores_ready, 1)

                def transpose_probs(n):
                    pe.wait_ge(probs_ready, count(a, HEADS, n + 1))
                    if due(count(a, HEADS, n - 1)):
                        pe.wait_ge(probsT_copied, count(a, HEADS, n - 1))
                    for j in range(KT):
                        mm = nc.tensor.transpose(psum[0:KP, T_BANKS[n % 2], j * TOK:(j + 1) * TOK],
                                                 probs[:, n % RING, j * KP:(j + 1) * KP], ident[0:TOK, 0:TOK])
                    mm.then_inc(probsT_ready, 1)

                def weigh_values(quad):
                    c, odd = quad // 2, quad % 2
                    pe.wait_ge(probsT_copied, count(a, HEADS, 4 * quad + 4))
                    if quad == 0:
                        pe.wait_ge(dve_proj.sem, dve_proj.to("v2", a))
                        if due(dve_join.to("attnT", o)):
                            pe.wait_ge(dve_join.sem, dve_join.to("attnT", o))
                    for t in range(KT):
                        for j in range(4):
                            pair = 4 * c + j
                            mm = nc.tensor.matmul(
                                o_bank[32 * j:32 * j + 32, c * TOK:(c + 1) * TOK],
                                v_sb[k][:, t, pair, odd:odd + 2, :].rearrange("p e d -> p (e d)"),
                                probsT[:, (4 * quad + j) % TRING, t * TOK:(t + 1) * TOK],
                                start=(odd == 0 and t == 0), stop=(odd == 1 and t == KT - 1),
                                tile_position=(0, 32 * j), skip_group_check=True)
                    mm.then_inc(pv_done, 1)

                def product(name, bank):
                    mm = None
                    if name == "xT":
                        pe.wait_ge(x_in[k], turn(s, 1))
                        for c in range(DC):
                            mm = nc.tensor.transpose(bank[:, c * TOK:(c + 1) * TOK],
                                                     x_sb[k][:, c * 128:(c + 1) * 128], ident[0:TOK, 0:TOK])
                    elif name == "Sc":
                        pe.wait_ge(act_self.sem, act_self.to("xT", s))
                        for c in range(DC):
                            mm = nc.tensor.matmul(bank[0:TOK, 0:TOK], xT[:, c, :], xT[:, c, :],
                                                  start=(c == 0), stop=(c == DC - 1))
                    elif name == "PT":
                        pe.wait_ge(dve_self.sem, dve_self.to("sparse", s))
                        mm = nc.tensor.transpose(bank[0:TOK, 0:TOK], sparse[:, :], ident[0:TOK, 0:TOK])
                    elif name == "att":
                        pe.wait_ge(act_self.sem, act_self.to("sparseT", s))
                        mm = nc.tensor.matmul(bank[0:TOK, 0:DIM], sparseT[:, :], x_sb[k][:, :],
                                              start=True, stop=True)
                    elif name == "x1T":
                        pe.wait_ge(dve_self.sem, dve_self.to("x1", p))
                        for c in range(DC):
                            mm = nc.tensor.transpose(bank[:, c * TOK:(c + 1) * TOK],
                                                     x1[1 - k][:, c * 128:(c + 1) * 128], ident[0:TOK, 0:TOK])
                    elif name in ("c0", "c1"):
                        c = int(name[1])
                        pe.wait_ge(ctx_in[1 - k], turn(p, 1))
                        for j in range(KT):
                            mm = nc.tensor.transpose(bank[:, j * KP:(j + 1) * KP],
                                                     ctx_sb[1 - k][:, j, c * 128:(c + 1) * 128], ident[0:KP, 0:KP])
                    elif name == "qT":
                        pe.wait_ge(act_proj.sem, act_proj.to("x1T", p))
                        for r in range(DC):
                            for c in range(DC):
                                mm = nc.tensor.matmul(bank[:, r * TOK:(r + 1) * TOK],
                                                      wq_sb[:, c, r * 128:(r + 1) * 128], x1T[:, c, :],
                                                      start=(c == 0), stop=(c == DC - 1))
                    elif name in ("K0", "K1"):
                        r = int(name[1])
                        pe.wait_ge(dve_proj.sem, dve_proj.to("ctx_lo1", p))
                        if it == -1 and r == 0:
                            pe.wait_ge(setup_dve, 8)
                        for n, (c, w_part, x_part) in enumerate(
                                (c, *parts) for c in range(DC)
                                for parts in ((wk_hi, ctx_hi), (wk_lo, ctx_hi), (wk_hi, ctx_lo))):
                            mm = nc.tensor.matmul(bank[:, 0:KEYS_EVEN], w_part[:, c, r * 128:(r + 1) * 128],
                                                  x_part[:, c, :], start=(n == 0), stop=(n == 3 * DC - 1))
                    elif name in ("V0", "V1", "V2"):
                        j = int(name[1])
                        for n, (c, x_part, w_part) in enumerate(
                                (c, *parts) for c in range(DC)
                                for parts in ((ctx_hi, wv_hi), (ctx_hi, wv_lo), (ctx_lo, wv_hi))):
                            mm = nc.tensor.matmul(bank[0:KP, 0:DIM], x_part[:, c, j * KP:(j + 1) * KP],
                                                  w_part[:, c, :], start=(n == 0), stop=(n == 3 * DC - 1))
                    elif name == "rb":
                        pe.wait_ge(dve_attn.sem, dve_attn.to("rden_wide", o))
                        pe.wait_ge(act_join.sem, act_join.to("o_sb", o))
                        for c in range(DC):
                            mm = nc.tensor.matmul(
                                bank[:, c * TOK:(c + 1) * TOK],
                                rden_wide[:, CHUNK_HEADS * c:CHUNK_HEADS * (c + 1), :].rearrange("q h d -> q (h d)"),
                                ident[0:TOK, 0:TOK], start=True, stop=True)
                    elif name == "Wo":
                        pe.wait_ge(dve_join.sem, dve_join.to("attnT", o))
                        for c in range(DC):
                            mm = nc.tensor.matmul(bank[0:TOK, 0:DIM], attnT[:, c * TOK:(c + 1) * TOK],
                                                  wo_sb[:, c, :], start=(c == 0), stop=(c == DC - 1))
                    elif name == "x2T":
                        pe.wait_ge(dve_join.sem, dve_join.to("x2", o))
                        for c in range(DC):
                            mm = nc.tensor.transpose(bank[:, c * TOK:(c + 1) * TOK],
                                                     x2[1 - k][:, c * 128:(c + 1) * 128], ident[0:TOK, 0:TOK])
                    elif name[0] == "T":
                        if name == "T0":
                            pe.wait_ge(wi_in[p[1]], 32)
                        e = EXPERTS_PER * p[1] + int(name[1])
                        for c in range(DC):
                            for r in range(DC):
                                mm = nc.tensor.transpose(bank[:, c * DIM + r * 128:c * DIM + (r + 1) * 128],
                                                         wi_sb[:, e, r, c * 128:(c + 1) * 128], ident)
                    elif name[0] == "E":
                        j = int(name[1])
                        pe.wait_ge(act_weights.sem, act_weights.to(f"wiT{j}", p))
                        for r in range(DC):
                            for c in range(DC):
                                mm = nc.tensor.matmul(
                                    bank[:, r * DIM:(r + 1) * DIM],
                                    wiT[:, j % 2, c, r * 128:(r + 1) * 128],
                                    wout_sb[:, EXPERTS_PER * p[1] + j, c, :],
                                    start=(c == 0), stop=(c == DC - 1))
                    else:
                        if it == 1 and name == "lg":
                            pe.wait_ge(setup_dve, 10)
                        if it == 2 and name == "m0":
                            pe.wait_ge(dve_weights.sem, dve_weights.to(f"we_lo{EXPERTS_PER - 1}", o))
                        if name == "lg":
                            pe.wait_ge(dve_join.sem, dve_join.to("x2_lo", o))
                            hi, lo = x2_hi[1 - k], x2_lo[1 - k]
                            w_hi, w_lo, width = wr_hi[:, :, :], wr_lo[:, :, :], EXPERTS
                        else:
                            n, width, hi, lo = int(name[1]), 2 * DIM, x2_hi[k], x2_lo[k]
                            w_hi = we_hi[:, :, n * width:(n + 1) * width]
                            w_lo = we_lo[:, :, n * width:(n + 1) * width]
                        parts = [(c, x_part, w_part) for c in range(DC)
                                 for x_part, w_part in ((hi, w_hi), (hi, w_lo), (lo, w_hi))]
                        for n, (c, x_part, w_part) in enumerate(parts):
                            mm = nc.tensor.matmul(bank[0:TOK, 0:width], x_part[:, c, :], w_part[:, c, :],
                                                  start=(n == 0), stop=(n == len(parts) - 1))
                    return mm

                for n in range(SLOTS):
                    if attn and 0 < n < HEADS - 1:
                        scores(a, n + 1)
                    if n >= SLOTS - 2 and active("attn", it + 1):
                        scores(p, n - (SLOTS - 2))
                    if attn and 2 <= n < HEADS + 2:
                        transpose_probs(n - 2)
                    for u, (name, slot, _) in enumerate(ALL_USES):
                        if slot != n or not active(STAGE_OF[name], it):
                            continue
                        before = previous_use(u, it)
                        if before:
                            steps, step = taken[before[0]]
                            pe.wait_ge(steps[STAGE_OF[before[0]]].sem, steps[STAGE_OF[before[0]]].to(step, shift(at, before[1])))
                        product(name, bank_of[name]).then_inc(pe_steps[STAGE_OF[name]].did(name), 1)
                    if it == FIRST and n == 5:
                        transpose_attn_w()
                    if it == FIRST and n == 12:
                        sum_attn_w()
                    if attn and n >= 7 and (n - 7) % 4 == 0:
                        weigh_values((n - 7) // 4)
                if it == FIRST:
                    pe.wait_ge(weights_in, 16 * WEIGHTS)

            run(pe, iteration)


_INS = [("x", "x"), ("ctx_1024", "context"), ("mask_Bx1xSxS2_bk1", "mask"), ("L0_attn_W", "attn_w"),
        ("L0_xattn_Wq", "wq"), ("L0_xattn_bq", "bq"), ("L0_xattn_Wk", "wk"), ("L0_xattn_bk", "bk"),
        ("L0_xattn_Wv", "wv"), ("L0_xattn_bv", "bv"), ("L0_xattn_Wo", "wo"), ("L0_xattn_bo", "bo"),
        ("L0_ffn_Wr", "wr"), ("L0_ffn_Wi", "wi"), ("L0_ffn_Wo", "wout")]


def kernel(**inputs):
    import numpy as np
    import concourse.bacc as bacc
    from concourse.bass_utils import run_bass_kernel_spmd

    nc = bacc.Bacc("TRN2", target_bir_lowering=False, num_devices=1)
    arrays, args = {}, {}
    for name, short in _INS:
        a = np.ascontiguousarray(inputs[name])
        if name.startswith("mask"):
            a = a.reshape(BATCH, TOK, KEYS)
        arrays[f"in_{short}"] = a
    consts = np.zeros((128, 128 + 2 + EXPERTS), np.float32)
    consts[:, 0:128] = np.eye(128, dtype=np.float32)
    for half in range(2):
        rows = np.arange(128) // HEAD_DIM % 2 == half
        consts[rows, 128 + half] = -Q_SCALE
    consts[:, 130:] = np.arange(EXPERTS, dtype=np.float32)
    arrays["in_consts"] = consts
    for key, a in arrays.items():
        args[key[3:]] = nc.dram_tensor(key, a.shape, mybir.dt.from_np(a.dtype), kind="ExternalInput").ap()
    out = nc.dram_tensor("out_dram", (BATCH, TOK, DIM), fp32, kind="ExternalOutput").ap()
    decoder_layer(nc, **args, out=out)
    r = run_bass_kernel_spmd(nc, [arrays], core_ids=[0])
    return r.results[0]["out_dram"]
```
